# Optimizing a Trainium2 kernel written in Bass

```python
import numpy as np
import jax
import jax.numpy as jnp

def _softmax(x, axis=-1):
    return jax.nn.softmax(x, axis=axis)

def _gelu(x):
    return jax.nn.gelu(x, approximate=True)

def _silu(x):
    return jax.nn.silu(x)

def _sigmoid(x):
    return jax.nn.sigmoid(x)

def _layernorm(x, axis=-1, eps=1e-05):
    m = jnp.mean(x, axis=axis, keepdims=True)
    v = jnp.var(x, axis=axis, keepdims=True)
    return (x - m) / jnp.sqrt(v + eps)

def _scatter_add(tgt, idx, src, axis=0):
    return tgt.at[idx].add(src)

def _segment_sum(src, seg, n):
    return jax.ops.segment_sum(src, seg, n)
kernel_name = 'mk_conv_seq_d2_conv_nhwc256_r2_cebbaa'

def setup_inputs(seed: int=0):
    np.random.seed(seed)
    _w = jnp.asarray

    def _rec_inputs():
        import jax
        import jax.numpy as jnp
        _gk = jax.random.key(seed)
        x = -7.109e-05 + 0.9999 * jax.random.normal(jax.random.fold_in(_gk, 1), (4, 128, 128, 128), jnp.float32)
        return x
    x = _rec_inputs()

    def _L0_conv_setup():
        import jax, jax.numpy as jnp
        import numpy as np
        from jax import lax
        B, H, W, C = (4, 128, 128, 128)
        LN_EPS = 0.001
        key = jax.random.key(seed)
        ks = jax.random.split(key, 9)
        s1 = 1.0 / np.sqrt(C)
        s3 = 1.0 / np.sqrt(9 * C)
        return {'x': jax.random.normal(ks[0], (B, H, W, C), dtype=jnp.float32), 'w_h': jax.random.normal(ks[1], (C, C), dtype=jnp.float32) * s1, 'b_h': jnp.zeros((C,), dtype=jnp.float32), 'w_l': jax.random.normal(ks[2], (C, C), dtype=jnp.float32) * s1, 'b_l': jnp.zeros((C,), dtype=jnp.float32), 'w_f': jax.random.normal(ks[3], (3, 3, C, C), dtype=jnp.float32) * s3, 'b_f': jnp.zeros((C,), dtype=jnp.float32), 'gamma': jnp.ones((C,), dtype=jnp.float32), 'beta': jnp.zeros((C,), dtype=jnp.float32)}
    _L0_conv_all = _L0_conv_setup()
    _L0_conv_in = {k: v for k, v in _L0_conv_all.items() if k in ('w_h', 'b_h', 'w_l', 'b_l', 'w_f', 'b_f', 'gamma', 'beta')}
    del _L0_conv_all

    def _L1_conv_setup():
        import jax, jax.numpy as jnp
        import numpy as np
        EMB = 128
        D_INNER = 256
        HEADDIM = 32
        NHEADS = D_INNER // HEADDIM
        DSTATE = 64
        DCONV = 4
        CONV_DIM = D_INNER + 2 * DSTATE
        D_IN_PROJ = 2 * D_INNER + 2 * DSTATE + NHEADS
        LN_EPS = 1e-05

        def _layernorm(x, w, b):
            m = jnp.mean(x, axis=-1, keepdims=True)
            v = jnp.mean((x - m) ** 2, axis=-1, keepdims=True)
            return (x - m) * jax.lax.rsqrt(v + LN_EPS) * w + b

        def _wn_linear(x, g, v, b):
            w = g[:, None] * v / jnp.linalg.norm(v, axis=1, keepdims=True)
            return x @ w.T + b

        def _ssm_scan(x, dt, A, Bm, Cm):
            dA = jnp.exp(dt * A)
            dtx = dt[..., None] * x
            bsz = x.shape[0]

            def step(h, inp):
                dA_t, dtx_t, B_t, C_t = inp
                h = h * dA_t[:, :, None, None] + dtx_t[..., None] * B_t[:, None, None, :]
                y = jnp.einsum('bhpn,bn->bhp', h, C_t)
                return (h, y)
            h0 = jnp.zeros((bsz, NHEADS, HEADDIM, DSTATE), x.dtype)
            xs = (jnp.swapaxes(dA, 0, 1), jnp.swapaxes(dtx, 0, 1), jnp.swapaxes(Bm, 0, 1), jnp.swapaxes(Cm, 0, 1))
            _, ys = jax.lax.scan(step, h0, xs)
            return jnp.swapaxes(ys, 0, 1)

        def _mamba2(u, in_proj_w, conv_w, conv_b, dt_bias, A_log, D_param, ssm_norm_w, out_proj_w):
            B, L, _ = u.shape
            zxbcdt = u @ in_proj_w.T
            z_gate = zxbcdt[..., :D_INNER]
            xBC = zxbcdt[..., D_INNER:D_INNER + CONV_DIM]
            dt = zxbcdt[..., D_INNER + CONV_DIM:]
            xp = jnp.pad(xBC, ((0, 0), (DCONV - 1, 0), (0, 0)))
            xc = jax.lax.conv_general_dilated(jnp.swapaxes(xp, 1, 2), conv_w[:, None, :], (1,), 'VALID', feature_group_count=CONV_DIM, dimension_numbers=('NCH', 'OIH', 'NCH'))
            xc = jax.nn.silu(jnp.swapaxes(xc, 1, 2) + conv_b)
            x = xc[..., :D_INNER].reshape(B, L, NHEADS, HEADDIM)
            Bm = xc[..., D_INNER:D_INNER + DSTATE]
            Cm = xc[..., D_INNER + DSTATE:]
            dt = jax.nn.softplus(dt + dt_bias)
            A = -jnp.exp(A_log)
            y = _ssm_scan(x, dt, A, Bm, Cm) + D_param[None, None, :, None] * x
            y = y.reshape(B, L, D_INNER)
            yg = y * jax.nn.silu(z_gate)
            yn = yg * jax.lax.rsqrt(jnp.mean(yg ** 2, axis=-1, keepdims=True) + LN_EPS) * ssm_norm_w
            return yn @ out_proj_w.T
        key = jax.random.key(seed)
        ks = jax.random.split(key, 12)
        B, NU, NA = (1, 32, 256)

        def rn(k, shape, scale):
            return jax.random.normal(k, shape, dtype=jnp.float32) * scale
        z = rn(ks[0], (B, NU, NA, EMB), 1.0)
        in_proj_w = rn(ks[1], (D_IN_PROJ, EMB), EMB ** (-0.5))
        conv_w = rn(ks[2], (CONV_DIM, DCONV), DCONV ** (-0.5))
        conv_b = rn(ks[3], (CONV_DIM,), 0.02)
        dt_bias = jnp.log(jnp.expm1(jax.random.uniform(ks[4], (NHEADS,), minval=0.001, maxval=0.1)))
        A_log = jnp.log(jax.random.uniform(ks[5], (NHEADS,), minval=1.0, maxval=16.0))
        D_param = jnp.ones((NHEADS,), dtype=jnp.float32)
        ssm_norm_w = jnp.ones((D_INNER,), dtype=jnp.float32)
        out_proj_w = rn(ks[6], (EMB, D_INNER), D_INNER ** (-0.5))
        ff_v = rn(ks[7], (EMB, EMB), EMB ** (-0.5))
        ff_g = jnp.linalg.norm(ff_v, axis=1)
        ff_b = jnp.zeros((EMB,), dtype=jnp.float32)
        fc1_v = rn(ks[8], (EMB, EMB), EMB ** (-0.5))
        fc1_g = jnp.linalg.norm(fc1_v, axis=1)
        fc1_b = jnp.zeros((EMB,), dtype=jnp.float32)
        fc2_v = rn(ks[9], (EMB, EMB), EMB ** (-0.5))
        fc2_g = jnp.linalg.norm(fc2_v, axis=1)
        fc2_b = jnp.zeros((EMB,), dtype=jnp.float32)
        return {'z': z, 'ln1_w': jnp.ones((EMB,), dtype=jnp.float32), 'ln1_b': jnp.zeros((EMB,), dtype=jnp.float32), 'in_proj_w': in_proj_w, 'conv_w': conv_w, 'conv_b': conv_b, 'dt_bias': dt_bias, 'A_log': A_log, 'D_param': D_param, 'ssm_norm_w': ssm_norm_w, 'out_proj_w': out_proj_w, 'ff_g': ff_g, 'ff_v': ff_v, 'ff_b': ff_b, 'ln2_w': jnp.ones((EMB,), dtype=jnp.float32), 'ln2_b': jnp.zeros((EMB,), dtype=jnp.float32), 'fc1_g': fc1_g, 'fc1_v': fc1_v, 'fc1_b': fc1_b, 'fc2_g': fc2_g, 'fc2_v': fc2_v, 'fc2_b': fc2_b}
    _L1_conv_all = _L1_conv_setup()
    _L1_conv_in = {k: v for k, v in _L1_conv_all.items() if k in ('ln1_w', 'ln1_b', 'in_proj_w', 'conv_w', 'conv_b', 'dt_bias', 'A_log', 'D_param', 'ssm_norm_w', 'out_proj_w', 'ff_g', 'ff_v', 'ff_b', 'ln2_w', 'ln2_b', 'fc1_g', 'fc1_v', 'fc1_b', 'fc2_g', 'fc2_v', 'fc2_b')}
    del _L1_conv_all
    return {'x': x, 'L0_conv_w_h': _L0_conv_in['w_h'], 'L0_conv_b_h': _L0_conv_in['b_h'], 'L0_conv_w_l': _L0_conv_in['w_l'], 'L0_conv_b_l': _L0_conv_in['b_l'], 'L0_conv_w_f': _L0_conv_in['w_f'], 'L0_conv_b_f': _L0_conv_in['b_f'], 'L0_conv_gamma': _L0_conv_in['gamma'], 'L0_conv_beta': _L0_conv_in['beta'], 'L1_conv_ln1_w': _L1_conv_in['ln1_w'], 'L1_conv_ln1_b': _L1_conv_in['ln1_b'], 'L1_conv_in_proj_w': _L1_conv_in['in_proj_w'], 'L1_conv_conv_w': _L1_conv_in['conv_w'], 'L1_conv_conv_b': _L1_conv_in['conv_b'], 'L1_conv_dt_bias': _L1_conv_in['dt_bias'], 'L1_conv_A_log': _L1_conv_in['A_log'], 'L1_conv_D_param': _L1_conv_in['D_param'], 'L1_conv_ssm_norm_w': _L1_conv_in['ssm_norm_w'], 'L1_conv_out_proj_w': _L1_conv_in['out_proj_w'], 'L1_conv_ff_g': _L1_conv_in['ff_g'], 'L1_conv_ff_v': _L1_conv_in['ff_v'], 'L1_conv_ff_b': _L1_conv_in['ff_b'], 'L1_conv_ln2_w': _L1_conv_in['ln2_w'], 'L1_conv_ln2_b': _L1_conv_in['ln2_b'], 'L1_conv_fc1_g': _L1_conv_in['fc1_g'], 'L1_conv_fc1_v': _L1_conv_in['fc1_v'], 'L1_conv_fc1_b': _L1_conv_in['fc1_b'], 'L1_conv_fc2_g': _L1_conv_in['fc2_g'], 'L1_conv_fc2_v': _L1_conv_in['fc2_v'], 'L1_conv_fc2_b': _L1_conv_in['fc2_b']}

def reference(x, L0_conv_w_h, L0_conv_b_h, L0_conv_w_l, L0_conv_b_l, L0_conv_w_f, L0_conv_b_f, L0_conv_gamma, L0_conv_beta, L1_conv_ln1_w, L1_conv_ln1_b, L1_conv_in_proj_w, L1_conv_conv_w, L1_conv_conv_b, L1_conv_dt_bias, L1_conv_A_log, L1_conv_D_param, L1_conv_ssm_norm_w, L1_conv_out_proj_w, L1_conv_ff_g, L1_conv_ff_v, L1_conv_ff_b, L1_conv_ln2_w, L1_conv_ln2_b, L1_conv_fc1_g, L1_conv_fc1_v, L1_conv_fc1_b, L1_conv_fc2_g, L1_conv_fc2_v, L1_conv_fc2_b):
    import jax
    import jax.numpy as jnp

    def _L0_conv_ref(x, w_h, b_h, w_l, b_l, w_f, b_f, gamma, beta):
        import jax, jax.numpy as jnp
        import numpy as np
        from jax import lax
        B, H, W, C = (4, 128, 128, 128)
        LN_EPS = 0.001
        xc = x.astype(jnp.complex64)
        xc = jnp.transpose(xc, (0, 3, 1, 2))
        f = jnp.fft.fft2(xc, axes=(-2, -1))
        f = jnp.fft.fftshift(f, axes=(-2, -1))
        amp = jnp.abs(f)
        phase = jnp.angle(f)
        amp = jnp.transpose(amp, (0, 2, 3, 1))
        phase = jnp.transpose(phase, (0, 2, 3, 1))
        gate_h = jax.nn.sigmoid(jnp.einsum('bhwc,cd->bhwd', amp, w_h) + b_h)
        gate_l = jax.nn.sigmoid(jnp.einsum('bhwc,cd->bhwd', amp, w_l) + b_l)
        mod_amp = amp * gate_h + amp * gate_l
        rec = lax.complex(mod_amp * jnp.cos(phase), mod_amp * jnp.sin(phase))
        rec = jnp.fft.ifftshift(rec, axes=(1, 2))
        rec = jnp.transpose(rec, (0, 3, 1, 2))
        spatial = jnp.real(jnp.fft.ifft2(rec, axes=(-2, -1)))
        spatial = jnp.transpose(spatial, (0, 2, 3, 1))
        conv = lax.conv_general_dilated(spatial, w_f, window_strides=(1, 1), padding='SAME', dimension_numbers=('NHWC', 'HWIO', 'NHWC')) + b_f
        fused = jax.nn.swish(conv)
        y = fused + x
        mean = jnp.mean(y, axis=-1, keepdims=True)
        var = jnp.var(y, axis=-1, keepdims=True)
        y = (y - mean) * lax.rsqrt(var + LN_EPS)
        return y * gamma + beta

    def _L1_conv_ref(z, ln1_w, ln1_b, in_proj_w, conv_w, conv_b, dt_bias, A_log, D_param, ssm_norm_w, out_proj_w, ff_g, ff_v, ff_b, ln2_w, ln2_b, fc1_g, fc1_v, fc1_b, fc2_g, fc2_v, fc2_b):
        import jax, jax.numpy as jnp
        import numpy as np
        EMB = 128
        D_INNER = 256
        HEADDIM = 32
        NHEADS = D_INNER // HEADDIM
        DSTATE = 64
        DCONV = 4
        CONV_DIM = D_INNER + 2 * DSTATE
        D_IN_PROJ = 2 * D_INNER + 2 * DSTATE + NHEADS
        LN_EPS = 1e-05

        def _layernorm(x, w, b):
            m = jnp.mean(x, axis=-1, keepdims=True)
            v = jnp.mean((x - m) ** 2, axis=-1, keepdims=True)
            return (x - m) * jax.lax.rsqrt(v + LN_EPS) * w + b

        def _wn_linear(x, g, v, b):
            w = g[:, None] * v / jnp.linalg.norm(v, axis=1, keepdims=True)
            return x @ w.T + b

        def _ssm_scan(x, dt, A, Bm, Cm):
            dA = jnp.exp(dt * A)
            dtx = dt[..., None] * x
            bsz = x.shape[0]

            def step(h, inp):
                dA_t, dtx_t, B_t, C_t = inp
                h = h * dA_t[:, :, None, None] + dtx_t[..., None] * B_t[:, None, None, :]
                y = jnp.einsum('bhpn,bn->bhp', h, C_t)
                return (h, y)
            h0 = jnp.zeros((bsz, NHEADS, HEADDIM, DSTATE), x.dtype)
            xs = (jnp.swapaxes(dA, 0, 1), jnp.swapaxes(dtx, 0, 1), jnp.swapaxes(Bm, 0, 1), jnp.swapaxes(Cm, 0, 1))
            _, ys = jax.lax.scan(step, h0, xs)
            return jnp.swapaxes(ys, 0, 1)

        def _mamba2(u, in_proj_w, conv_w, conv_b, dt_bias, A_log, D_param, ssm_norm_w, out_proj_w):
            B, L, _ = u.shape
            zxbcdt = u @ in_proj_w.T
            z_gate = zxbcdt[..., :D_INNER]
            xBC = zxbcdt[..., D_INNER:D_INNER + CONV_DIM]
            dt = zxbcdt[..., D_INNER + CONV_DIM:]
            xp = jnp.pad(xBC, ((0, 0), (DCONV - 1, 0), (0, 0)))
            xc = jax.lax.conv_general_dilated(jnp.swapaxes(xp, 1, 2), conv_w[:, None, :], (1,), 'VALID', feature_group_count=CONV_DIM, dimension_numbers=('NCH', 'OIH', 'NCH'))
            xc = jax.nn.silu(jnp.swapaxes(xc, 1, 2) + conv_b)
            x = xc[..., :D_INNER].reshape(B, L, NHEADS, HEADDIM)
            Bm = xc[..., D_INNER:D_INNER + DSTATE]
            Cm = xc[..., D_INNER + DSTATE:]
            dt = jax.nn.softplus(dt + dt_bias)
            A = -jnp.exp(A_log)
            y = _ssm_scan(x, dt, A, Bm, Cm) + D_param[None, None, :, None] * x
            y = y.reshape(B, L, D_INNER)
            yg = y * jax.nn.silu(z_gate)
            yn = yg * jax.lax.rsqrt(jnp.mean(yg ** 2, axis=-1, keepdims=True) + LN_EPS) * ssm_norm_w
            return yn @ out_proj_w.T
        b, nu, na, e = z.shape
        u = _layernorm(z, ln1_w, ln1_b).reshape(-1, na, e)
        y = _mamba2(u, in_proj_w, conv_w, conv_b, dt_bias, A_log, D_param, ssm_norm_w, out_proj_w)
        y = _wn_linear(y, ff_g, ff_v, ff_b).reshape(b, nu, na, e)
        z = z + y
        h = _layernorm(z, ln2_w, ln2_b)
        h = jax.nn.gelu(_wn_linear(h, fc1_g, fc1_v, fc1_b), approximate=False)
        h = _wn_linear(h, fc2_g, fc2_v, fc2_b)
        return z + h

    def _gn(v, G=32, eps=1e-05):
        B_, H_, W_, C_ = v.shape
        g = v.reshape(B_, H_, W_, G, C_ // G)
        m = jnp.mean(g, axis=(1, 2, 4), keepdims=True)
        s = jnp.var(g, axis=(1, 2, 4), keepdims=True)
        return ((g - m) / jnp.sqrt(s + eps)).reshape(v.shape)

    def _ln_c(v, eps=1e-06):
        m = jnp.mean(v, axis=-1, keepdims=True)
        s = jnp.var(v, axis=-1, keepdims=True)
        return (v - m) / jnp.sqrt(s + eps)

    def _ln_t(v, eps=1e-05):
        m = jnp.mean(v, axis=-1, keepdims=True)
        s = jnp.var(v, axis=-1, keepdims=True)
        return (v - m) / jnp.sqrt(s + eps)

    def _to_tokens(v):
        B_, H_, W_, C_ = v.shape
        return v.reshape(B_, H_ * W_, C_)

    def _from_tokens(t, like):
        return t.reshape(like.shape)
    x = _L0_conv_ref(x, L0_conv_w_h, L0_conv_b_h, L0_conv_w_l, L0_conv_b_l, L0_conv_w_f, L0_conv_b_f, L0_conv_gamma, L0_conv_beta)
    x = _L1_conv_ref(x, L1_conv_ln1_w, L1_conv_ln1_b, L1_conv_in_proj_w, L1_conv_conv_w, L1_conv_conv_b, L1_conv_dt_bias, L1_conv_A_log, L1_conv_D_param, L1_conv_ssm_norm_w, L1_conv_out_proj_w, L1_conv_ff_g, L1_conv_ff_v, L1_conv_ff_b, L1_conv_ln2_w, L1_conv_ln2_b, L1_conv_fc1_g, L1_conv_fc1_v, L1_conv_fc1_b, L1_conv_fc2_g, L1_conv_fc2_v, L1_conv_fc2_b)
    return x

_drawn_inputs = setup_inputs


def setup_inputs(seed=0):
    import zlib

    import numpy as np

    out = dict(_drawn_inputs(seed))
    spreads = {'L0_conv_b_h': (0.0, 2.0),
     'L0_conv_b_l': (0.0, 2.0),
     'L0_conv_b_f': (0.0, 0.1),
     'L0_conv_gamma': (1.0, 0.2),
     'L0_conv_beta': (0.0, 0.1),
     'L1_conv_ln1_w': (1.0, 0.2),
     'L1_conv_ln1_b': (0.0, 0.1),
     'L1_conv_D_param': (1.0, 0.2),
     'L1_conv_ssm_norm_w': (1.0, 0.2),
     'L1_conv_ff_b': (0.0, 0.1),
     'L1_conv_ln2_w': (1.0, 0.2),
     'L1_conv_ln2_b': (0.0, 0.1),
     'L1_conv_fc1_b': (0.0, 0.1),
     'L1_conv_fc2_b': (0.0, 0.1)}
    factors = {'L1_conv_conv_b': 3.66}
    for name, (base, spread) in spreads.items():
        noise = np.random.default_rng([zlib.crc32(name.encode()), seed]).standard_normal(out[name].shape)
        drawn = base * np.exp(spread * noise) if base else spread * noise
        out[name] = jnp.asarray(drawn.astype(out[name].dtype))
    for name, factor in factors.items():
        out[name] = (out[name] * factor).astype(out[name].dtype)
    return out
```

```python
from contextlib import ExitStack

import concourse.bass as bass
from concourse import mybir
from concourse.bass import ds

FP = mybir.dt.float32
FR = mybir.dt.float32r
BF = mybir.dt.bfloat16
ALU = mybir.AluOpType
ACT = mybir.ActivationFunctionType

P = 128
IMAGES, H, W, C = 4, 128, 128, 128
QUADS = IMAGES * H // 4
STRIP = H // 2
SROWS, SCOLS = STRIP + 2, W + 2
HALF = H // 2
HEADS, HEADDIM, DSTATE, DINNER = 8, 32, 64, 256
BIG = 1e30
EPS0, EPS1 = 1e-3, 1e-5
TINY = 1e-30
SBUF_START = 16640


class Place:

    def __init__(self, nc, tag, at=SBUF_START):
        self.nc, self.tag, self.at = nc, tag, at

    def __call__(self, name, shape, dt=FP):
        size = 2 if dt == BF else 4
        for n in shape[1:]:
            size *= n
        at = self.at
        self.at = (at + size + 63) // 64 * 64
        return self.nc.alloc_sbuf_tensor_at(self.tag + name, shape, dt, offset=at)


def eight_columns(sp, t, b, rows, g):
    return [t[ds(sp.snap(b), 1), rows, ds(sp.snap(g * 8 + 4 * e), 4), :].rearrange("o r w c -> (o r) (w c)")
            for e in range(2)]


def spectral_block(nc, a, z1):
    ctx = ExitStack()
    with ctx:
        def sem(name):
            return ctx.enter_context(nc.semaphore(name))

        def sems(name, n):
            return [sem(f"{name}{i}") for i in range(n)]

        sb = Place(nc, "f_")
        spec_at = sb.at
        spec = sb("spec", [P, 3 * HALF, C])
        rowspec = sb("rowspec", [P, P, C])
        work = sb("work", [P, 8, 512])
        xt = sb("xt", [P, 4, 512])
        edge = sb("edge", [P, 4, C])
        edge_amp = sb("edge_amp", [P, 2, C])
        dft_h, cosm, sinm, nsinm, ident, wh, wl, gamma, beta = (
            sb(n, [P, P]) for n in ("dft_h", "cosm", "sinm", "nsinm", "ident", "wh", "wl", "gamma", "beta"))
        idft_h = sb("idft_h", [P, H + 2])
        bias = sb("bias", [P, 3])
        wf_hi = sb("wf_hi", [P, 9, C], FR)
        wf_lo = sb("wf_lo", [P, 9, C], FR)
        stats = sb("stats", [P, 2, 4, 6])
        mv = sb("mv", [P, 2, 4, 2])
        rstd = sb("rstd", [P, 2, 4])
        mhalf = sb("mhalf", [P, 4])
        over = Place(nc, "f_", spec_at)
        s_hi = over("s_hi", [P, SCOLS, SROWS], FR)
        s_lo = over("s_lo", [P, SCOLS, SROWS], FR)
        conv_v = over("conv_v", [P, 2, 512])
        xres = over("xres", [P, 2, 512])
        ysum = over("ysum", [P, 2, 512])
        zout = over("zout", [P, 2, 512])
        wf_raw = over("wf_raw", [P, 9, C])

        ps = ctx.enter_context(nc.psum_tensor("f_ps", [P, 8, 512], FP))

        waited = sem("f_waited")
        consts_in, wf_in = sem("f_consts_in"), sem("f_wf_in")
        wf_hi_ready, wf_ready, mhalf_ready = sem("f_wf_hi_ready"), sem("f_wf_ready"), sem("f_mhalf_ready")
        x_in, y_mm, y_free = sems("f_x_in", 4), sems("f_y_mm", 4), sems("f_y_free", 4)
        f_mm, re_ready, im_ready, im_sq, ss_ready, amp_ready = (
            sems("f_" + n, 2) for n in ("f_mm", "re_ready", "im_ready", "im_sq", "ss_ready", "amp_ready"))
        edge_mm, edge_copied, edge_sq, edge_ss, edge_amp_ready = (
            sem("f_" + n) for n in ("edge_mm", "edge_copied", "edge_sq", "edge_ss", "edge_amp_ready"))
        ampT_mm, ampT_ready, gate_mm, sig_ready, gsum_ready, gT_mm, gated, neg_done, edge_scaled = (
            sem("f_" + n) for n in ("ampT_mm", "ampT_ready", "gate_mm", "sig_ready", "gsum_ready",
                                    "gT_mm", "gated", "neg_done", "edge_scaled"))
        t_mm, t_free = sem("f_t_mm"), sems("f_t_free", 4)
        s_mm, hi_ready, lo_ready, pad_ready = (sem("f_" + n) for n in ("s_mm", "hi_ready", "lo_ready", "pad_ready"))
        conv_mm, silu_done, vT_mm, ysum_done, stats_done, mv_ready, var_eps, rstd_ready, scaled, z_ready = (
            sems("f_" + n, 2) for n in ("conv_mm", "silu_done", "vT_mm", "ysum_done", "stats_done",
                                        "mv_ready", "var_eps", "rstd_ready", "scaled", "z_ready"))
        xres_in, z_out = sems("f_xres_in", 2), sems("f_z_out", 2)

        GROUPS = HALF // 4
        G17 = GROUPS + 1
        NCONST = 16 * 13

        block = ctx.enter_context(nc.Block())

        @block.sync
        def _(sp):
            for one in z_out:
                sp.sem_inc(one)
            for t, src in ((dft_h, a["dft_h"]), (cosm, a["cosm"]), (sinm, a["sinm"]), (nsinm, a["nsinm"]),
                           (ident, a["ident"]), (wh, a["w_h"]), (wl, a["w_l"]), (idft_h, a["idft_h"])):
                sp.dma_start(t[:, :], src).then_inc(consts_in, 16)
            for n, src in enumerate((a["b_h"], a["b_l"], a["b_f"])):
                sp.dma_start(bias[:, n:n + 1], src.rearrange("(p o) -> p o", o=1)).then_inc(consts_in, 16)
            sp.dma_start(gamma[:, :], a["gamma"].partition_broadcast(P)).then_inc(consts_in, 16)
            sp.dma_start(beta[:, :], a["beta"].partition_broadcast(P)).then_inc(consts_in, 16)
            sp.dma_start(wf_raw[:, :, :], a["w_f"].rearrange("t c d -> c t d")).then_inc(wf_in, 16)
            with sp.Fori(0, IMAGES) as b:
                with sp.Fori(0, 8) as t:
                    for j in range(4):
                        src = a["x_cols"][ds(sp.snap(b * 32 + t * 4 + j), 1)].rearrange("o h n -> h (o n)")
                        free = sp.snap(b * 8 + t + 1)
                        sp.wait_ge(y_mm[j], free)
                        sp.dma_start(xt[:, j, :], src).then_inc(x_in[j], 16)
                done = sp.snap(b * 32 + 32)
                sp.wait_ge(t_mm, done)
                sp.sem_inc(waited)
                for strip in range(2):
                    rows = slice(strip * STRIP, (strip + 1) * STRIP)
                    for s in range(2):
                        srcs = eight_columns(sp, a["x"], b, rows, s)
                        use = sp.snap(b * 16 + (strip * 8 + 1))
                        sp.wait_ge(ysum_done[s], use)
                        for e in range(2):
                            sp.dma_start(xres[e * STRIP:(e + 1) * STRIP, s, :], srcs[e]).then_inc(xres_in[s], 16)
                    with sp.Fori(0, 7) as j:
                        for s in range(2):
                            srcs = eight_columns(sp, a["x"], b, rows, j * 2 + (s + 2))
                            dsts = eight_columns(sp, z1, b, rows, j * 2 + s)
                            use = sp.snap(b * 16 + (strip * 8 + 1) + j)
                            added = sp.snap(b * 16 + (strip * 8 + 2) + j)
                            sp.wait_ge(ysum_done[s], added)
                            for e in range(2):
                                sp.dma_start(xres[e * STRIP:(e + 1) * STRIP, s, :], srcs[e]).then_inc(xres_in[s], 16)
                            sp.wait_ge(z_ready[s], use)
                            for e in range(2):
                                sp.dma_start(dsts[e], zout[e * STRIP:(e + 1) * STRIP, s, :]).then_inc(z_out[s], 16)
                    for s in range(2):
                        dsts = eight_columns(sp, z1, b, rows, 14 + s)
                        use = sp.snap(b * 16 + (strip * 8 + 8))
                        sp.wait_ge(z_ready[s], use)
                        for e in range(2):
                            sp.dma_start(dsts[e], zout[e * STRIP:(e + 1) * STRIP, s, :]).then_inc(z_out[s], 16)
            for s in range(2):
                sp.wait_ge(z_out[s], 32 * IMAGES * 16 + 1)

        @block.tensor
        def _(pe):
            def conv(use, r, s):
                pe.wait_ge(silu_done[s], use + 1)
                for tap in range(9):
                    ky, kx = tap // 3, tap % 3
                    hi = s_hi[:, ds(r * 8 + kx, 8), ky:ky + STRIP]
                    lo = s_lo[:, ds(r * 8 + kx, 8), ky:ky + STRIP]
                    out = ps[:, 4 + s, :].rearrange("p (w r) -> p w r", w=8)
                    pe.matmul(out, wf_hi[:, tap, :], hi, start=(tap == 0), stop=False)
                    pe.matmul(out, wf_hi[:, tap, :], lo, start=False, stop=False)
                    mm = pe.matmul(out, wf_lo[:, tap, :], hi, start=False, stop=(tap == 8))
                mm.then_inc(conv_mm[s], 1)

            def turn(use, s):
                pe.wait_ge(silu_done[s], use + 2)
                pe.wait_ge(ysum_done[s], use + 1)
                for k in range(4):
                    mm = pe.transpose(ps[:, 6 + s, k * P:(k + 1) * P], conv_v[:, s, k * P:(k + 1) * P], ident[:, :])
                mm.then_inc(vT_mm[s], 1)

            pe.wait_ge(consts_in, NCONST)
            pe.wait_ge(wf_ready, 1)
            for one in (*y_mm, *vT_mm):
                pe.sem_inc(one)
            with pe.Fori(0, IMAGES) as b:
                for s in range(2):
                    pe.wait_ge(silu_done[s], b * 16 + 1)
                    pe.wait_ge(ysum_done[s], b * 16 + 1)
                pe.sem_inc(waited)
                with pe.Fori(0, 8) as t:
                    for j in range(4):
                        pe.wait_ge(x_in[j], b * 128 + t * 16 + 16)
                        pe.wait_ge(y_free[j], b * 8 + t + 1)
                        for c in range(4):
                            mm = pe.matmul(ps[:, j, c * P:(c + 1) * P], xt[:, j, c * P:(c + 1) * P], dft_h[:, :],
                                           start=True, stop=True)
                        mm.then_inc(y_mm[j], 1)
                for j in range(4):
                    pe.wait_ge(y_free[j], b * 8 + 9)
                pe.sem_inc(waited)
                with pe.Fori(0, GROUPS // 2) as q:
                    for s in range(2):
                        pe.wait_ge(re_ready[s], b * 8 + q + 1)
                        pe.wait_ge(im_ready[s], b * 8 + q + 1)
                        y_re = rowspec[:, ds(q * 8 + s * 4, 4), :]
                        y_im = rowspec[:, ds(q * 8 + s * 4 + HALF, 4), :]
                        out_re = ps[:, 2 * s, :].rearrange("p (r c) -> p r c", r=4)
                        out_im = ps[:, 2 * s + 1, :].rearrange("p (r c) -> p r c", r=4)
                        pe.matmul(out_re, cosm[:, :], y_re, start=True, stop=False)
                        pe.matmul(out_im, cosm[:, :], y_im, start=True, stop=False)
                        pe.matmul(out_re, sinm[:, :], y_im, start=False, stop=True)
                        pe.matmul(out_im, nsinm[:, :], y_re, start=False, stop=True).then_inc(f_mm[s], 1)
                for n, (w, row) in enumerate(((cosm, 0), (nsinm, 0), (sinm, HALF), (cosm, HALF))):
                    mm = pe.matmul(ps[:, 4, n * P:(n + 1) * P], w[:, :], rowspec[:, row, :], start=True, stop=True)
                mm.then_inc(edge_mm, 1)
                for s in range(2):
                    pe.wait_ge(amp_ready[s], b * 8 + 9)
                    pe.wait_ge(re_ready[s], b * 8 + 9)
                    pe.wait_ge(im_ready[s], b * 8 + 9)
                for q in range(G17 + 2):
                    if q < G17:
                        if q >= 2:
                            pe.wait_ge(ampT_ready, b * G17 + (q - 1))
                        if q == GROUPS:
                            pe.wait_ge(edge_amp_ready, b + 1)
                        for k in range(4 if q < GROUPS else 2):
                            src = spec[:, 4 * q + k, :] if q < GROUPS else edge_amp[:, k, :]
                            mm = pe.transpose(ps[:, q % 2, k * P:(k + 1) * P], src, ident[:, :])
                        mm.then_inc(ampT_mm, 1)
                    if 1 <= q <= G17:
                        g = q - 1
                        n = 512 if g < GROUPS else 256
                        pe.wait_ge(ampT_ready, b * G17 + (g + 1))
                        if g >= 2:
                            pe.wait_ge(sig_ready, b * G17 + (g - 1))
                        if g == 1:
                            pe.wait_ge(edge_copied, b + 1)
                            pe.wait_ge(edge_sq, b + 1)
                        for w, bank in ((wh, 2), (wl, 3)):
                            mm = pe.matmul(ps[:, bank + 2 * (g % 2), 0:n], w[:, :], work[:, g % 2, 0:n],
                                           start=True, stop=True)
                        mm.then_inc(gate_mm, 1)
                    if q >= 2:
                        g = q - 2
                        pe.wait_ge(gsum_ready, b * G17 + (g + 1))
                        if g >= 2:
                            pe.wait_ge(gated, b * G17 + (g - 1))
                        for k in range(4 if g < GROUPS else 2):
                            mm = pe.transpose(ps[:, 6 + g % 2, k * P:(k + 1) * P],
                                              work[:, 6 + g % 2, k * P:(k + 1) * P], ident[:, :])
                        mm.then_inc(gT_mm, 1)
                pe.wait_ge(gated, b * G17 + G17)
                pe.wait_ge(neg_done, b * G17 + G17)
                for j in range(C // 4):
                    if j >= 4:
                        pe.wait_ge(t_free[j % 4], b * 8 + j // 4)
                    for k in range(4):
                        out = ps[:, j % 4, k * P:(k + 1) * P]
                        pe.matmul(out, spec[:, HALF:3 * HALF, 4 * j + k], cosm[:, :], start=True, stop=False)
                        mm = pe.matmul(out, spec[:, 0:2 * HALF, 4 * j + k], sinm[:, :], start=False, stop=True)
                    mm.then_inc(t_mm, 1)
                for j in range(4):
                    pe.wait_ge(t_free[j], b * 8 + 8)
                for strip in range(2):
                    for j in range(W // 8):
                        if j >= 2:
                            pe.wait_ge(lo_ready, b * 32 + (strip * 16 + j - 1))
                        for k in range(8):
                            mm = pe.matmul(ps[:, 2 * (j % 2) + k // 4, (k % 4) * SROWS:(k % 4 + 1) * SROWS],
                                           rowspec[:, :, 8 * j + k], idft_h[:, strip * STRIP:strip * STRIP + SROWS],
                                           start=True, stop=True)
                        mm.then_inc(s_mm, 1)
                    pe.wait_ge(lo_ready, b * 32 + (strip * 16 + 16))
                    pe.wait_ge(pad_ready, b * 2 + 2)
                    use = b * 16 + strip * 8
                    conv(use, 0, 0)
                    with pe.Fori(0, 7) as j:
                        conv(b * 16 + strip * 8 + j, j * 2 + 1, 1)
                        turn(b * 16 + strip * 8 + j, 0)
                        conv(b * 16 + (strip * 8 + 1) + j, j * 2 + 2, 0)
                        turn(b * 16 + strip * 8 + j, 1)
                    conv(b * 16 + (strip * 8 + 7), 15, 1)
                    turn(b * 16 + (strip * 8 + 7), 0)
                    turn(b * 16 + (strip * 8 + 7), 1)

        @block.scalar
        def _(act):
            act.wait_ge(consts_in, NCONST)
            act.wait_ge(wf_in, 16)
            act.activation(wf_hi[:, :, :], wf_raw[:, :, :], ACT.Copy).then_inc(wf_hi_ready, 1)
            for one in (y_free[0], y_free[2], *re_ready, *amp_ready, *silu_done):
                act.sem_inc(one)
            with act.Fori(0, IMAGES) as b:
                with act.Fori(0, 8) as t:
                    for j in (0, 2):
                        act.wait_ge(y_mm[j], b * 8 + t + 2)
                        act.activation(rowspec[:, :, ds(t * 16 + 4 * j, 4)].rearrange("p k c -> p c k"),
                                       ps[:, j, :].rearrange("p (c k) -> p c k", c=4), ACT.Copy).then_inc(y_free[j], 1)
                act.preload_act_table(ACT.Sqrt)
                with act.Fori(0, GROUPS // 2) as q:
                    for s in range(2):
                        act.wait_ge(f_mm[s], b * 8 + q + 1)
                        act.activation(spec[:, ds(q * 8 + s * 4 + HALF, 4), :],
                                       ps[:, 2 * s, :].rearrange("p (r c) -> p r c", r=4), ACT.Copy)
                        act.activation(work[:, 2 * s, :], ps[:, 2 * s, :], ACT.Square).then_inc(re_ready[s], 1)
                        act.wait_ge(ss_ready[s], b * 8 + q + 1)
                        act.activation(spec[:, ds(q * 8 + s * 4, 4), :],
                                       work[:, 4 + s, :].rearrange("p (r c) -> p r c", r=4),
                                       ACT.Sqrt).then_inc(amp_ready[s], 1)
                act.wait_ge(edge_mm, b + 1)
                act.activation(work[:, 6, :], ps[:, 4, :], ACT.Square).then_inc(edge_sq, 1)
                act.wait_ge(edge_ss, b + 1)
                act.activation(edge_amp[:, :, :], work[:, 7, 0:256].rearrange("p (r c) -> p r c", r=2),
                               ACT.Sqrt).then_inc(edge_amp_ready, 1)
                for g in range(G17):
                    n = 512 if g < GROUPS else 256
                    act.wait_ge(gate_mm, b * G17 + (g + 1))
                    if g >= 2:
                        act.wait_ge(gsum_ready, b * G17 + (g - 1))
                    for k in range(2):
                        ins = act.activation(work[:, 2 + 2 * (g % 2) + k, 0:n], ps[:, 2 + 2 * (g % 2) + k, 0:n],
                                             ACT.Sigmoid, bias=bias[:, k:k + 1])
                    ins.then_inc(sig_ready, 1)
                for j in range(0, C // 4, 2):
                    act.wait_ge(t_mm, b * 32 + (j + 1))
                    act.activation(rowspec[:, 4 * j:4 * j + 4, :],
                                   ps[:, j % 4, :].rearrange("p (c w) -> p c w", c=4), ACT.Copy).then_inc(t_free[j % 4], 1)
                for strip in range(2):
                    for j in range(W // 8):
                        act.wait_ge(s_mm, b * 32 + (strip * 16 + j + 1))
                        act.activation(s_hi[:, 1 + 8 * j:9 + 8 * j, :].rearrange("p (b w) r -> p b w r", b=2),
                                       ps[:, 2 * (j % 2):2 * (j % 2) + 2, 0:4 * SROWS]
                                       .rearrange("p b (w r) -> p b w r", r=SROWS), ACT.Copy).then_inc(hi_ready, 1)
                    act.preload_act_table(ACT.Silu)
                    with act.Fori(0, 8) as j:
                        for s in range(2):
                            act.wait_ge(conv_mm[s], b * 16 + (strip * 8 + 1) + j)
                            act.wait_ge(vT_mm[s], b * 16 + strip * 8 + j + 1)
                            act.activation(conv_v[:, s, :].rearrange("p (k e r) -> p e k r", k=4, e=2),
                                           ps[:, 4 + s, :].rearrange("p (e k r) -> p e k r", k=4, e=2), ACT.Silu,
                                           bias=bias[:, 2:3]).then_inc(silu_done[s], 1)

        @block.vector
        def _(dve):
            dve.wait_ge(consts_in, NCONST)
            dve.wait_ge(wf_hi_ready, 1)
            dve.tensor_tensor(wf_lo[:, :, :], wf_raw[:, :, :], wf_hi[:, :, :].bitcast(FP), ALU.subtract).then_inc(wf_ready, 1)
            for one in (y_free[1], y_free[3], *im_ready, *ysum_done):
                dve.sem_inc(one)
            with dve.Fori(0, IMAGES) as b:
                with dve.Fori(0, 8) as t:
                    for j in (1, 3):
                        dve.wait_ge(y_mm[j], b * 8 + t + 2)
                        dve.tensor_copy(rowspec[:, :, ds(t * 16 + 4 * j, 4)].rearrange("p k c -> p c k"),
                                        ps[:, j, :].rearrange("p (c k) -> p c k", c=4)).then_inc(y_free[j], 1)
                for s in range(2):
                    dve.wait_ge(z_out[s], b * 512 + 1)
                dve.sem_inc(waited)
                with dve.Fori(0, GROUPS // 2) as q:
                    for s in range(2):
                        dve.wait_ge(f_mm[s], b * 8 + q + 1)
                        im = spec[:, ds(q * 8 + s * 4 + 2 * HALF, 4), :]
                        dve.tensor_copy(im, ps[:, 2 * s + 1, :].rearrange("p (r c) -> p r c", r=4)).then_inc(im_ready[s], 1)
                        dve.wait_ge(im_ready[s], b * 8 + q + 2)
                        dve.tensor_tensor(work[:, 2 * s + 1, :].rearrange("p (r c) -> p r c", r=4), im, im,
                                          ALU.mult).then_inc(im_sq[s], 1)
                        dve.wait_ge(im_sq[s], b * 8 + q + 1)
                        dve.wait_ge(re_ready[s], b * 8 + q + 2)
                        dve.wait_ge(amp_ready[s], b * 8 + q + 1)
                        dve.scalar_tensor_tensor(out=work[:, 4 + s, :], in0=work[:, 2 * s, :], scalar=TINY,
                                                 in1=work[:, 2 * s + 1, :], op0=ALU.max, op1=ALU.add).then_inc(ss_ready[s], 1)
                dve.wait_ge(edge_sq, b + 1)
                dve.tensor_copy(edge[:, :, :], ps[:, 4, :].rearrange("p (r c) -> p r c", r=4)).then_inc(edge_copied, 1)
                pairs = work[:, 6, :].rearrange("p (k r c) -> p k r c", k=2, r=2)
                dve.scalar_tensor_tensor(out=work[:, 7, 0:256].rearrange("p (k c) -> p k c", k=2), in0=pairs[:, :, 0, :],
                                         scalar=TINY, in1=pairs[:, :, 1, :], op0=ALU.max, op1=ALU.add).then_inc(edge_ss, 1)
                for q in range(G17 + 2):
                    if q < G17:
                        n = 512 if q < GROUPS else 256
                        dve.wait_ge(ampT_mm, b * G17 + (q + 1))
                        if q >= 2:
                            dve.wait_ge(gate_mm, b * G17 + (q - 1))
                        dve.tensor_copy(work[:, q % 2, 0:n], ps[:, q % 2, 0:n]).then_inc(ampT_ready, 1)
                    if 1 <= q <= G17:
                        g = q - 1
                        n = 512 if g < GROUPS else 256
                        dve.wait_ge(sig_ready, b * G17 + (g + 1))
                        if g >= 2:
                            dve.wait_ge(gT_mm, b * G17 + (g - 1))
                        dve.tensor_tensor(work[:, 6 + g % 2, 0:n], work[:, 2 + 2 * (g % 2), 0:n],
                                          work[:, 3 + 2 * (g % 2), 0:n], ALU.add).then_inc(gsum_ready, 1)
                    if q >= 2:
                        g = q - 2
                        dve.wait_ge(gT_mm, b * G17 + (g + 1))
                        gate = ps[:, 6 + g % 2, :].rearrange("p (r c) -> p r c", r=4)
                        if g < GROUPS:
                            for row in (HALF + 4 * g, 2 * HALF + 4 * g):
                                part = spec[:, row:row + 4, :]
                                ins = dve.tensor_tensor(part, part, gate, ALU.mult)
                            ins.then_inc(gated, 1)
                        else:
                            for k in range(2):
                                part = edge[:, 2 * k:2 * k + 2, :]
                                ins = dve.tensor_tensor(part, part, gate[:, k:k + 1, :].to_broadcast([P, 2, C]), ALU.mult)
                            ins.then_inc(edge_scaled, 1)
                            dve.wait_ge(edge_scaled, b + 1)
                            dve.tensor_tensor(spec[:, HALF:3 * HALF:HALF, :], edge[:, 0:2, :], edge[:, 2:4, :],
                                              ALU.add).then_inc(gated, 1)
                for j in range(1, C // 4, 2):
                    dve.wait_ge(t_mm, b * 32 + (j + 1))
                    dve.tensor_copy(rowspec[:, 4 * j:4 * j + 4, :],
                                    ps[:, j % 4, :].rearrange("p (c w) -> p c w", c=4)).then_inc(t_free[j % 4], 1)
                for strip in range(2):
                    for j in range(W // 8):
                        dve.wait_ge(hi_ready, b * 32 + (strip * 16 + j + 1))
                        cols = (slice(None), slice(1 + 8 * j, 9 + 8 * j), slice(None))
                        dve.tensor_tensor(s_lo[cols].rearrange("p (b w) r -> p b w r", b=2),
                                          ps[:, 2 * (j % 2):2 * (j % 2) + 2, 0:4 * SROWS]
                                          .rearrange("p b (w r) -> p b w r", r=SROWS),
                                          s_hi[cols].bitcast(FP).rearrange("p (b w) r -> p b w r", b=2),
                                          ALU.subtract).then_inc(lo_ready, 1)
                    with dve.Fori(0, 8) as j:
                        for s in range(2):
                            use = b * 16 + strip * 8 + j
                            dve.wait_ge(vT_mm[s], use + 2)
                            dve.wait_ge(xres_in[s], b * 512 + (strip * 256 + 32) + j * 32)
                            dve.tensor_tensor(ysum[:, s, :], ps[:, 6 + s, :], xres[:, s, :], ALU.add).then_inc(ysum_done[s], 1)
                            dve.wait_ge(ysum_done[s], use + 2)
                            for r in range(4):
                                ins = dve.bn_stats(stats[:, s, r, :], ysum[:, s, r * P:(r + 1) * P])
                            ins.then_inc(stats_done[s], 1)
                            dve.wait_ge(stats_done[s], use + 1)
                            dve.sem_inc(waited)
                            for r in range(4):
                                ins = dve.bn_aggr(mv[:, s, r, :], stats[:, s, r, :])
                            ins.then_inc(mv_ready[s], 1)
                            dve.wait_ge(mv_ready[s], use + 1)
                            dve.wait_ge(z_out[s], b * 512 + strip * 256 + j * 32 + 1)
                            for r in range(4):
                                ins = dve.scalar_tensor_tensor(out=zout[:, s, r * P:(r + 1) * P], in0=ysum[:, s, r * P:(r + 1) * P],
                                                               scalar=mv[:, s, r, 0:1], in1=gamma[:, :],
                                                               op0=ALU.subtract, op1=ALU.mult)
                            ins.then_inc(scaled[s], 1)
                            dve.wait_ge(scaled[s], use + 1)
                            dve.wait_ge(rstd_ready[s], use + 1)
                            for r in range(4):
                                ins = dve.scalar_tensor_tensor(out=zout[:, s, r * P:(r + 1) * P], in0=zout[:, s, r * P:(r + 1) * P],
                                                               scalar=rstd[:, s, r:r + 1], in1=beta[:, :],
                                                               op0=ALU.mult, op1=ALU.add)
                            ins.then_inc(z_ready[s], 1)

        @block.gpsimd
        def _(pool):
            pool.memset(mhalf[:, :], -0.5).then_inc(mhalf_ready, 1)
            pool.wait_ge(mhalf_ready, 1)
            with pool.Fori(0, IMAGES) as b:
                for g in range(G17):
                    pool.wait_ge(gated, b * G17 + (g + 1))
                    pool.sem_inc(waited)
                    first, last = (max(4 * g, 1), 4 * g + 4) if g < GROUPS else (0, 1)
                    pool.tensor_scalar(spec[:, first:last, :], spec[:, 2 * HALF + first:2 * HALF + last, :], -1.0, 1.0,
                                       ALU.mult, ALU.mult).then_inc(neg_done, 1)
                pool.wait_ge(t_mm, b * 32 + 32)
                pool.sem_inc(waited)
                for t in (s_hi, s_lo):
                    pool.memset(t[:, 0:SCOLS:SCOLS - 1, :].bitcast(FP), 0.0).then_inc(pad_ready, 1)
                for strip in range(2):
                    with pool.Fori(0, 8) as j:
                        for s in range(2):
                            use = b * 16 + strip * 8 + j
                            pool.wait_ge(mv_ready[s], use + 1)
                            pool.sem_inc(waited)
                            pool.tensor_scalar(rstd[:, s, :], mv[:, s, :, 1], EPS0, None, ALU.add).then_inc(var_eps[s], 1)
                            pool.wait_ge(var_eps[s], use + 1)
                            pool.tensor_tensor(rstd[:, s, :], rstd[:, s, :], mhalf[:, :], ALU.pow).then_inc(rstd_ready[s], 1)


def dft_tables():
    import numpy as np
    n = np.arange(P)
    angle = 2 * np.pi * np.outer(n, n) / P
    cos, sin = (np.where(abs(m) < 1e-9, 0.0, m) for m in (np.cos(angle), np.sin(angle)))
    alt = (-1.0) ** n
    dft_h = np.concatenate([cos[:, :HALF], alt[:, None], -sin[:, 1:HALF]], axis=1)
    inv = np.zeros((P, H + 2))
    scale = 1.0 / (H * W)
    inv[0, 1:H + 1] = scale
    inv[1:HALF, 1:H + 1] = 2 * scale * cos[1:HALF]
    inv[HALF, 1:H + 1] = scale * alt
    inv[HALF + 1:, 1:H + 1] = -2 * scale * sin[1:HALF]
    f = lambda m: np.ascontiguousarray(m, dtype=np.float32)
    return {"dft_h": f(dft_h), "cosm": f(cos), "sinm": f(sin), "nsinm": f(-sin), "idft_h": f(inv),
            "ident": f(np.eye(P))}


class Step:

    def __init__(self, n, half, parity):
        self.n, self.half, self.s = n, half, parity


def pipeline(engine, steps, body):
    head = 4

    def at(n):
        return Step(n, n // 2, n % 2) if 0 <= n < steps else None

    for n in range(head):
        body(at(n), at(n - 1), at(n - 2))
    with engine.Fori(head // 2, steps // 2) as m:
        for s in range(2):
            body(Step(m * 2 + s, m, s), Step(m * 2 + (s - 1), m + (s - 1), 1 - s), Step(m * 2 + (s - 2), m - 1, s))
    for n in range(steps, steps + 3):
        body(at(n), at(n - 1), at(n - 2))


def later(wait, sem, value):
    if not isinstance(value, int) or value > 0:
        wait(sem, value)


def four(t):
    return t.rearrange("p (g n) -> p g n", g=4)


def sequence_block(nc, a, z1, out):
    ctx = ExitStack()
    with ctx:
        def sem(name):
            return ctx.enter_context(nc.semaphore("g_" + name))

        def sems(name, n):
            return [sem(f"{name}{i}") for i in range(n)]

        HD = 4 * HEADS
        sb = Place(nc, "g_")
        ident, tri = sb("ident", [P, P]), sb("tri", [P, P])
        ident_b, mask_b = sb("ident_b", [P, P], BF), sb("mask_b", [P, P], BF)
        wx, wz, wdt = sb("wx", [P, 3 * P]), sb("wz", [P, 2 * P]), sb("wdt", [P, HEADS])
        conv_w, conv_b = sb("conv_w", [P, 3, 4]), sb("conv_b", [P, 3])
        lncol = sb("lncol", [P, 4])
        fc1_b = sb("fc1_b", [P, 1])
        dtb, alog, aexp = sb("dtb", [P, HEADS]), sb("alog", [P, HEADS]), sb("aexp", [P, HEADS])
        amat = sb("amat", [P, HD])
        dcol, diag = sb("dcol", [P, 2]), sb("diag", [P, 2, P])
        ssm_w, op_raw = sb("ssm_w", [P, 2]), sb("op_raw", [P, DINNER])
        vraw, gcol, vsq = sb("vraw", [P, 3, P]), sb("gcol", [P, 3]), sb("vsq", [P, 3])
        vn, wt = sb("vn", [P, 3, P]), sb("wt", [P, 3, P])
        wc = sb("wc", [P, 2, P])
        ffb, fc2b = sb("ffb", [P, P]), sb("fc2b", [P, P])
        mhalf = sb("mhalf", [P, HD])
        ind_h, ind_g, negm = sb("ind_h", [P, HEADS]), sb("ind_g", [P, 4]), sb("negm", [P, 1])
        zin, zres, outb = (sb(n, [P, 2, 4, P]) for n in ("zin", "zres", "outb"))
        zresb, u, z2, z2b, hn = (sb(n, [P, 4, P]) for n in ("zresb", "u", "z2", "z2b", "hn"))
        ut, ht, gl = (sb(n, [P, 4 * P]) for n in ("ut", "ht", "gl"))
        acc = sb("acc", [P, 3, 4, P])
        xs = sb("xs", [P, 2, 2, 4, P])
        bmat, cmat = sb("bmat", [DSTATE, 2, 4, P]), sb("cmat", [DSTATE, 2, 4, P])
        zs, yg = sb("zs", [P, 2, 4, DINNER]), sb("yg", [P, 2, 4, DINNER])
        v, vabs, ve, vu, vl, vr, vx = (sb(n, [P, HD]) for n in ("v", "vabs", "ve", "vu", "vl", "vr", "vx"))
        dt, dta = sb("dt", [P, 2, HD]), sb("dta", [P, 2, 4, HD])
        hi4, q = sb("hi4", [P, P], FR), sb("q", [P, P], FR)
        rz, l4 = sb("rz", [P, HEADS, P], FR), sb("l4", [P, 4, P], FR)
        emat, mmat = sb("emat", [P, 2, 8 * P]), sb("mmat", [P, 2, 8 * P])
        dtx = sb("dtx", [P, 2, 512])
        ygt = sb("ygt", [P, 4, 2, P])
        junk = sb("junk", [P, DINNER])
        ss, ry = sb("ss", [P, 2, 4]), sb("ry", [P, 2, 4])
        st1, st2, mv1, mv2 = sb("st1", [P, 4, 6]), sb("st2", [P, 4, 6]), sb("mv1", [P, 4, 2]), sb("mv2", [P, 4, 2])
        r1, r2 = sb("r1", [P, 4]), sb("r2", [P, 4])

        ps = ctx.enter_context(nc.psum_tensor("g_ps", [P, 8, 512], FP))

        waited = sem("waited")
        win = sem("win")
        const_p, const_d, const_a = sem("const_p"), sem("const_d"), sem("const_a")
        a_ready, vsq_ready, vrs_ready, vn_ready, wt_mm, wt_ready, wc_mm, wc_ready = (
            sem(n) for n in ("a_ready", "vsq_ready", "vrs_ready", "vn_ready", "wt_mm", "wt_ready", "wc_mm", "wc_ready"))
        zin_in, zres_in, out_done = sems("zin_in", 2), sems("zres_in", 2), sems("out_done", 2)
        zresb_p, z2b_p, r1a_p, r1_p, r2a_p, r2_p, rya_p, ry_p = (
            sem(n) for n in ("zresb_p", "z2b_p", "r1a_p", "r1_p", "r2a_p", "r2_p", "rya_p", "ry_p"))
        ygt_mm, d_mm, xt_mm, y_mm, x_mm, z_mm, cs_mm, cb_mm, ut_mm, o_mm, dt_mm, ht_mm, f1_mm, f2_mm = (
            sem(n) for n in ("ygt_mm", "d_mm", "xt_mm", "y_mm", "x_mm", "z_mm", "cs_mm", "cb_mm", "ut_mm", "o_mm",
                             "dt_mm", "ht_mm", "f1_mm", "f2_mm"))
        ygt_a, ut_a, e_a, tap_a, sq_a, ve_a, vl_a, ht_a, gl_a, xs_a, bc_a, zs_a = (
            sem(n) for n in ("ygt_a", "ut_a", "e_a", "tap_a", "sq_a", "ve_a", "vl_a", "ht_a", "gl_a", "xs_a", "bc_a", "zs_a"))
        hi4_d, q_d, rz_d, l4_d, st1_d, mv1_d, dtx_d, u_d, m_d, z2_d, st2_d, mv2_d = (
            sem(n) for n in ("hi4_d", "q_d", "rz_d", "l4_d", "st1_d", "mv1_d", "dtx_d", "u_d", "m_d", "z2_d", "st2_d",
                             "mv2_d"))
        v_d, vabs_d, conv_d, gate_d, vu_d, hn_d, vr_d, vx_d, dt_d, dta_d, fin_d = (
            sem(n) for n in ("v_d", "vabs_d", "conv_d", "gate_d", "vu_d", "hn_d", "vr_d", "vx_d", "dt_d", "dta_d", "fin_d"))

        def col(src):
            return src.rearrange("(p o) -> p o", o=1)

        loads = [(ident[:, :], a["ident"]), (tri[:, :], a["tri"]), (wx[:, :], a["in_proj_t"][:, 256:640]),
                 (wz[:, :], a["in_proj_t"][:, 0:256]), (wdt[:, :], a["in_proj_t"][:, 640:648]),
                 (conv_w[:, :, :], a["conv_w"].rearrange("(j p) k -> p j k", j=3)), (conv_b[:, :], a["conv_b3"]),
                 (dcol[:, :], a["d_cols"]), (ssm_w[:, :], a["ssm_w2"]),
                 (lncol[:, 0:1], col(a["ln1_w"])), (lncol[:, 1:2], col(a["ln1_b"])),
                 (lncol[:, 2:3], col(a["ln2_w"])), (lncol[:, 3:4], col(a["ln2_b"])), (fc1_b[:, :], col(a["fc1_b"])),
                 (dtb[:, :], a["dt_bias"].partition_broadcast(P)), (alog[:, :], a["A_log"].partition_broadcast(P)),
                 (op_raw[:, :], a["out_proj_w"]), (vraw[:, 0, :], a["ff_v"]), (vraw[:, 1, :], a["fc1_v"]),
                 (vraw[:, 2, :], a["fc2_v"]), (gcol[:, 0:1], col(a["ff_g"])), (gcol[:, 1:2], col(a["fc1_g"])),
                 (gcol[:, 2:3], col(a["fc2_g"])), (ffb[:, :], a["ff_b"].partition_broadcast(P)),
                 (fc2b[:, :], a["fc2_b"].partition_broadcast(P)), (ind_h[:, :], a["ind_h"]),
                 (ind_g[:, :], a["ind_g"]), (negm[:, :], a["negm"])]
        NLOADS = 16 * len(loads)
        rows = z1.rearrange("b h w c -> (b h) w c")

        block = ctx.enter_context(nc.Block())

        @block.sync
        def _(sp):
            for dst, src in loads:
                sp.dma_start(dst, src).then_inc(win, 16)

            def store(n, s):
                at, done = sp.snap(n), sp.snap(n + 1)
                sp.wait_ge(fin_d, done)
                sp.dma_start(out[ds(at, 1)].rearrange("o w n -> w (o n)"),
                             outb[:, s].rearrange("p g n -> p (g n)")).then_inc(out_done[s], 16)

            def load(dst, step, read, got):
                src = rows[ds(sp.snap(step.n * 4), 4)].rearrange("r w c -> w r c")
                if not isinstance(step.n, int) or step.n > 1:
                    value = sp.snap(step.n - 1)
                    sp.wait_ge(read, value)
                sp.dma_start(dst[:, step.s], src).then_inc(got[step.s], 16)

            def body(sa, _b, sc):
                if sa:
                    load(zin, sa, u_d, zin_in)
                if sc:
                    load(zres, sc, zresb_p, zres_in)
                    if not isinstance(sc.n, int) or sc.n > 0:
                        store(sc.n - 1, 1 - sc.s)
                if not sa and not sc:
                    store(QUADS - 1, 1)

            pipeline(sp, QUADS, body)
            for s in range(2):
                sp.wait_ge(out_done[s], 16 * QUADS // 2)

        @block.gpsimd
        def _(pool):
            pool.memset(mhalf[:, :], -0.5).then_inc(const_p, 1)
            pool.wait_ge(win, NLOADS)
            pool.tensor_copy(ident_b[:, :], ident[:, :]).then_inc(const_p, 1)
            pool.wait_ge(const_p, 2)
            pool.wait_ge(vsq_ready, 3)
            pool.tensor_tensor(vsq[:, :], vsq[:, :], mhalf[:, 0:3], ALU.pow).then_inc(vrs_ready, 1)
            pool.wait_ge(vrs_ready, 1)
            pool.tensor_tensor(gcol[:, :], gcol[:, :], vsq[:, :], ALU.mult).then_inc(vrs_ready, 1)

            def rsqrt(dst, src, scale, eps, src_sem, src_count, sum_sem, root_sem, n):
                pool.wait_ge(src_sem, src_count)
                pool.sem_inc(waited)
                if scale is None:
                    pool.tensor_scalar(dst, src, eps, None, ALU.add).then_inc(sum_sem, 1)
                else:
                    pool.tensor_scalar(dst, src, scale, eps, ALU.mult, ALU.add).then_inc(sum_sem, 1)
                pool.wait_ge(sum_sem, n + 1)
                pool.tensor_tensor(dst, dst, mhalf[:, 0:4], ALU.pow).then_inc(root_sem, 1)

            def body(sa, sb_, sc):
                if sc:
                    pool.wait_ge(zres_in[sc.s], sc.half * 16 + 16)
                    later(pool.wait_ge, z2_d, sc.n)
                    pool.tensor_tensor(zresb[:, :, :], zres[:, sc.s], ffb[:, :].unsqueeze(1).to_broadcast([P, 4, P]),
                                       ALU.add).then_inc(zresb_p, 1)
                if sa:
                    rsqrt(r1[:, :], mv1[:, :, 1], None, EPS1, mv1_d, sa.n + 1, r1a_p, r1_p, sa.n)
                if sc:
                    rsqrt(r2[:, :], mv2[:, :, 1], None, EPS1, mv2_d, sc.n + 1, r2a_p, r2_p, sc.n)
                    later(pool.wait_ge, fin_d, sc.n)
                    pool.tensor_tensor(z2b[:, :, :], z2[:, :, :], fc2b[:, :].unsqueeze(1).to_broadcast([P, 4, P]),
                                       ALU.add).then_inc(z2b_p, 1)
                if sb_:
                    rsqrt(ry[:, sb_.s, :], ss[:, sb_.s, :], 1.0 / DINNER, EPS1, sq_a, sb_.n * 4 + 4, rya_p, ry_p, sb_.n)

            pipeline(pool, QUADS, body)

        @block.tensor
        def _(pe):
            pe.wait_ge(win, NLOADS)
            pe.wait_ge(vn_ready, 3)
            for n in range(3):
                pe.transpose(ps[:, 0, n * P:(n + 1) * P], vn[:, n, :], ident[:, :]).then_inc(wt_mm, 1)
            pe.wait_ge(wt_ready, 1)
            for j in range(2):
                pe.matmul(ps[:, 1, j * P:(j + 1) * P], op_raw[:, j * P:(j + 1) * P], wt[:, 0, :],
                          start=True, stop=True).then_inc(wc_mm, 1)
            pe.wait_ge(wc_ready, 2)
            pe.wait_ge(const_p, 2)
            pe.wait_ge(const_d, 3)
            pe.wait_ge(const_a, 2)

            def turn_yg(c, half):
                if half == 0:
                    gates_done = c.n * 2 + 4
                    if isinstance(c.n, int):
                        gates_done = min(gates_done, 2 * QUADS)
                    pe.wait_ge(zs_a, gates_done)
                    pe.wait_ge(gate_d, c.n * 4 + 4)
                else:
                    pe.wait_ge(ygt_a, c.n * 2 + 1)
                for k in range(4):
                    g, j = 2 * half + k // 2, k % 2
                    mm = pe.transpose(ps[:, 0, k * P:(k + 1) * P], yg[:, c.s, g, j * P:(j + 1) * P], ident[:, :])
                mm.then_inc(ygt_mm, 1)

            def decays(b, g):
                if g == 0:
                    pe.wait_ge(rz_d, b.n + 1)
                    pe.wait_ge(l4_d, b.n + 1)
                later(pe.wait_ge, e_a, b.n * 4 + g)
                for half in range(2):
                    dst = four(ps[:, 4 + half, :])
                    pe.matmul(dst, l4[:, g, :], rz[:, 4 * half:4 * half + 4, :], start=True, stop=False)
                    mm = pe.matmul(dst, ident_b[:, :], mask_b[:, :].unsqueeze(1).to_broadcast([P, 4, P]),
                                   start=False, stop=True)
                mm.then_inc(d_mm, 1)

            def turn_x(b, pair):
                if pair == 0:
                    pe.wait_ge(xs_a, b.n + 1)
                    later(pe.wait_ge, dtx_d, b.n * 2)
                else:
                    pe.wait_ge(dtx_d, b.n * 2 + 1)
                for k in range(4):
                    mm = pe.transpose(ps[:, 7, k * P:(k + 1) * P], xs[:, b.s, k % 2, 2 * pair + k // 2, :], ident[:, :])
                mm.then_inc(xt_mm, 1)

            def mix(b, g):
                pe.wait_ge(m_d, b.n * 4 + (g + 1))
                pe.wait_ge(dtx_d, b.n * 2 + (g // 2 + 1))
                later(pe.wait_ge, gate_d, b.n * 4 + g)
                for j in range(2):
                    pe.matmul(ps[:, 6, j * P:(j + 1) * P], xs[:, b.s, j, g, :], diag[:, j, :], start=(j == 0), stop=False)
                for h in range(HEADS):
                    at = (g % 2) * DINNER + HEADDIM * h
                    mm = pe.matmul(ps[:, 6, HEADDIM * h:HEADDIM * (h + 1)], mmat[:, g % 2, h * P:(h + 1) * P],
                                   dtx[:, g // 2, at:at + HEADDIM], start=False, stop=(h == HEADS - 1))
                mm.then_inc(y_mm, 1)

            def project(j, bank):
                pe.matmul(ps[:, bank, :], wx[:, j * P:(j + 1) * P], ut[:, :], start=True, stop=True).then_inc(x_mm, 1)

            def gates(pair, bank):
                for k in range(2):
                    g = 2 * pair + k
                    mm = pe.matmul(ps[:, bank, k * DINNER:(k + 1) * DINNER], ut[:, g * P:(g + 1) * P], wz[:, :],
                                   start=True, stop=True)
                mm.then_inc(z_mm, 1)

            def body(sa, sb_, sc):
                if sb_:
                    pe.wait_ge(dta_d, sb_.n + 1)
                    later(pe.wait_ge, gate_d, sb_.n * 4)
                    pe.matmul(ps[:, 6, 0:P], dta[:, sb_.s].rearrange("p r n -> p (r n)"), tri[:, :],
                              start=True, stop=True).then_inc(cs_mm, 1)
                    pe.wait_ge(bc_a, sb_.n + 1)
                    later(pe.wait_ge, m_d, sb_.n * 4)
                    for g in range(4):
                        mm = pe.matmul(ps[:, 3, g * P:(g + 1) * P], bmat[:, sb_.s, g, :], cmat[:, sb_.s, g, :],
                                       start=True, stop=True)
                    mm.then_inc(cb_mm, 1)
                    turn_x(sb_, 0)
                if sc:
                    turn_yg(sc, 0)
                if sb_:
                    decays(sb_, 0)
                if sc:
                    turn_yg(sc, 1)
                    pe.wait_ge(ygt_a, sc.n * 2 + 2)
                if sa:
                    later(pe.wait_ge, zs_a, sa.n * 2)
                    pe.wait_ge(u_d, sa.n + 1)
                    for g in range(4):
                        mm = pe.transpose(ps[:, 0, g * P:(g + 1) * P], u[:, g, :], ident[:, :])
                    mm.then_inc(ut_mm, 1)
                if sc:
                    later(pe.wait_ge, fin_d, sc.n)
                    for g in range(4):
                        for j in range(2):
                            mm = pe.matmul(ps[:, 2, g * P:(g + 1) * P], ygt[:, g, j, :], wc[:, j, :],
                                           start=(j == 0), stop=(j == 1))
                    mm.then_inc(o_mm, 1)
                if sb_:
                    decays(sb_, 1)
                if sa:
                    pe.wait_ge(ut_a, sa.n + 1)
                    project(0, 1)
                if sb_:
                    mix(sb_, 0)
                if sa:
                    if sb_:
                        pe.wait_ge(dtx_d, sb_.n * 2 + 1)
                    for g in range(4):
                        mm = pe.matmul(ps[:, 7, HEADS * g:HEADS * (g + 1)], ut[:, g * P:(g + 1) * P], wdt[:, :],
                                       start=True, stop=True)
                    mm.then_inc(dt_mm, 1)
                    if sc:
                        pe.wait_ge(z2_d, sc.n + 1)
                    project(1, 2)
                if sb_:
                    decays(sb_, 2)
                    mix(sb_, 1)
                    if sa:
                        pe.wait_ge(v_d, sa.n + 1)
                    turn_x(sb_, 1)
                if sa:
                    pe.wait_ge(conv_d, sa.n * 9 + 3)
                    project(2, 1)
                if sb_:
                    decays(sb_, 3)
                if sc:
                    pe.wait_ge(hn_d, sc.n + 1)
                    for g in range(4):
                        mm = pe.transpose(ps[:, 0, g * P:(g + 1) * P], hn[:, g, :], ident[:, :])
                    mm.then_inc(ht_mm, 1)
                if sb_:
                    mix(sb_, 2)
                if sc:
                    if sa:
                        pe.wait_ge(conv_d, sa.n * 9 + 6)
                    pe.wait_ge(ht_a, sc.n + 1)
                    pe.matmul(ps[:, 2, :], wt[:, 1, :], ht[:, :], start=True, stop=True).then_inc(f1_mm, 1)
                if sa:
                    pe.wait_ge(conv_d, sa.n * 9 + 9)
                    gates(0, 1)
                if sb_:
                    mix(sb_, 3)
                if sc:
                    pe.wait_ge(gl_a, sc.n + 1)
                    for g in range(4):
                        mm = pe.matmul(ps[:, 2, g * P:(g + 1) * P], gl[:, g * P:(g + 1) * P], wt[:, 2, :],
                                       start=True, stop=True)
                    mm.then_inc(f2_mm, 1)
                if sa:
                    gates(1, 0)

            pipeline(pe, QUADS, body)

        @block.scalar
        def _(act):
            act.wait_ge(win, NLOADS)
            act.activation(aexp[:, :], alog[:, :], ACT.Exp).then_inc(a_ready, 1)
            for n in range(3):
                act.activation(vn[:, n, :], vraw[:, n, :], ACT.Square, accum_out=vsq[:, n:n + 1]).then_inc(vsq_ready, 1)
            act.wait_ge(wt_mm, 3)
            act.activation(wt[:, :, :].rearrange("p n k -> p (n k)"), ps[:, 0, 0:3 * P], ACT.Copy).then_inc(wt_ready, 1)
            act.wait_ge(wc_mm, 2)
            for j in range(2):
                act.activation(wc[:, j, :], ps[:, 1, j * P:(j + 1) * P], ACT.Copy, scale=ssm_w[:, j:j + 1]).then_inc(wc_ready, 1)
            act.activation(rz[64:P, :, :], ind_h[64:P, :].unsqueeze(2).to_broadcast([64, HEADS, P]),
                           ACT.Copy).then_inc(const_a, 1)
            act.activation(l4[0:64, :, :], ind_g[0:64, :].unsqueeze(2).to_broadcast([64, 4, P]),
                           ACT.Copy).then_inc(const_a, 1)

            def exps(b, g):
                act.wait_ge(d_mm, b.n * 4 + (g + 1))
                later(act.wait_ge, m_d, b.n * 4 + (g - 1))
                act.activation(emat[:, g % 2, :].rearrange("p (b n) -> p b n", b=2), ps[:, 4:6, :], ACT.Exp).then_inc(e_a, 1)

            def first_tap(a_, j, bank):
                act.wait_ge(x_mm, a_.n * 3 + (j + 1))
                act.activation(acc[:, j], four(ps[:, bank, :]), ACT.Identity, bias=conv_b[:, j:j + 1],
                               scale=conv_w[:, j, 3:4]).then_inc(tap_a, 1)

            def squares(b, g):
                act.wait_ge(gate_d, b.n * 4 + (g + 1))
                later(act.wait_ge, sq_a, b.n * 4 + g)
                act.activation(junk[:, :], yg[:, b.s, g, :], ACT.Square, accum_out=ss[:, b.s, g:g + 1]).then_inc(sq_a, 1)

            def body(sa, sb_, sc):
                if sc:
                    for half in range(2):
                        act.wait_ge(ygt_mm, sc.n * 2 + (half + 1))
                        act.activation(ygt[:, 2 * half:2 * half + 2].rearrange("p g j n -> p (g j n)"), ps[:, 0, :],
                                       ACT.Copy).then_inc(ygt_a, 1)
                act.preload_act_table_set("natural_log_exp_and_others")
                if sb_:
                    exps(sb_, 0)
                if sa:
                    act.wait_ge(ut_mm, sa.n + 1)
                    act.activation(ut[:, :], ps[:, 0, :], ACT.Identity, bias=lncol[:, 1:2], scale=lncol[:, 0:1]).then_inc(ut_a, 1)
                if sb_:
                    exps(sb_, 1)
                if sa:
                    first_tap(sa, 0, 1)
                if sb_:
                    exps(sb_, 2)
                if sa:
                    first_tap(sa, 1, 2)
                if sb_:
                    squares(sb_, 0)
                if sa:
                    act.wait_ge(vabs_d, sa.n + 1)
                    act.activation(ve[:, :], vabs[:, :], ACT.Exp, scale=-1.0).then_inc(ve_a, 1)
                if sb_:
                    exps(sb_, 3)
                if sa:
                    act.wait_ge(vu_d, sa.n + 1)
                    act.activation(vl[:, :], vu[:, :], ACT.Ln).then_inc(vl_a, 1)
                    first_tap(sa, 2, 1)
                if sc:
                    act.wait_ge(ht_mm, sc.n + 1)
                    act.activation(ht[:, :], ps[:, 0, :], ACT.Identity, bias=lncol[:, 3:4], scale=lncol[:, 2:3]).then_inc(ht_a, 1)
                if sb_:
                    squares(sb_, 1)
                if sc:
                    act.wait_ge(f1_mm, sc.n + 1)
                    act.activation(gl[:, :], ps[:, 2, :], ACT.Gelu, bias=fc1_b[:, :]).then_inc(gl_a, 1)
                if sb_:
                    squares(sb_, 2)
                if sa:
                    act.wait_ge(conv_d, sa.n * 9 + 9)
                    act.activation(xs[:, sa.s], acc[:, 0:2], ACT.Silu).then_inc(xs_a, 1)
                    act.activation(bmat[:, sa.s], acc[0:64, 2], ACT.Silu)
                    act.activation(cmat[:, sa.s], acc[64:P, 2], ACT.Silu).then_inc(bc_a, 1)
                    for pair, bank in ((0, 1), (1, 0)):
                        act.wait_ge(z_mm, sa.n * 2 + (pair + 1))
                        act.activation(zs[:, sa.s, 2 * pair:2 * pair + 2].rearrange("p g n -> p (g n)"), ps[:, bank, :],
                                       ACT.Silu).then_inc(zs_a, 1)
                if sb_:
                    squares(sb_, 3)

            pipeline(act, QUADS, body)

        @block.vector
        def _(dve):
            dve.wait_ge(win, NLOADS)
            dve.tensor_scalar(mask_b[:, :], tri[:, :], -1.0, BIG, ALU.add, ALU.mult).then_inc(const_d, 1)
            dve.wait_ge(a_ready, 1)
            dve.tensor_scalar(amat[:, :].rearrange("p (g h) -> p g h", g=4),
                              aexp[:, :].unsqueeze(1).to_broadcast([P, 4, HEADS]), -1.0, None, ALU.mult).then_inc(const_d, 1)
            for j in range(2):
                ins = dve.tensor_scalar(diag[:, j, :], ident[:, :], dcol[:, j:j + 1], None, ALU.mult)
            ins.then_inc(const_d, 1)
            dve.wait_ge(vrs_ready, 2)
            for n in range(3):
                dve.tensor_scalar(vn[:, n, :], vraw[:, n, :], gcol[:, n:n + 1], None, ALU.mult).then_inc(vn_ready, 1)
            dve.wait_ge(const_d, 3)
            dve.wait_ge(const_a, 2)

            def pair_dtx(b, pair):
                dve.wait_ge(xt_mm, b.n * 2 + (pair + 1))
                later(dve.wait_ge, y_mm, b.n * 4 + (2 * pair - 2))
                dve.tensor_tensor(dtx[:, pair, :].rearrange("p (n d) -> p n d", d=HEADDIM),
                                  ps[:, 7, :].rearrange("p (n d) -> p n d", d=HEADDIM),
                                  dt[:, b.s, 16 * pair:16 * pair + 16].unsqueeze(2).to_broadcast([P, 16, HEADDIM]),
                                  ALU.mult).then_inc(dtx_d, 1)

            def weigh(b, g):
                dve.wait_ge(e_a, b.n * 4 + (g + 1))
                dve.wait_ge(cb_mm, b.n + 1)
                later(dve.wait_ge, y_mm, b.n * 4 + (g - 1))
                dve.tensor_tensor(mmat[:, g % 2, :].rearrange("p (h n) -> p h n", h=HEADS),
                                  emat[:, g % 2, :].rearrange("p (h n) -> p h n", h=HEADS),
                                  ps[:, 3, g * P:(g + 1) * P].unsqueeze(1).to_broadcast([P, HEADS, P]),
                                  ALU.mult).then_inc(m_d, 1)

            def taps(a_, j, bank):
                dve.wait_ge(tap_a, a_.n * 3 + (j + 1))
                for k in range(1, 4):
                    if k >= 2:
                        dve.wait_ge(conv_d, a_.n * 9 + (3 * j + k - 1))
                    dve.scalar_tensor_tensor(out=acc[:, j, :, k:], in0=four(ps[:, bank, :])[:, :, 0:P - k],
                                             scalar=conv_w[:, j, 3 - k:4 - k], in1=acc[:, j, :, k:],
                                             op0=ALU.mult, op1=ALU.add).then_inc(conv_d, 1)

            def gate(b, g):
                dve.wait_ge(y_mm, b.n * 4 + (g + 1))
                dve.wait_ge(zs_a, b.n * 2 + 2)
                dve.tensor_tensor(yg[:, b.s, g, :], ps[:, 6, 0:DINNER], zs[:, b.s, g, :], ALU.mult).then_inc(gate_d, 1)

            def moments(src, st, mv, st_sem, mv_sem, n):
                for g in range(4):
                    ins = dve.bn_stats(st[:, g, :], src[:, g, :])
                ins.then_inc(st_sem, 1)
                dve.wait_ge(st_sem, n + 1)
                dve.sem_inc(waited)
                for g in range(4):
                    ins = dve.bn_aggr(mv[:, g, :], st[:, g, :])
                ins.then_inc(mv_sem, 1)

            def norm(dst, src, mv, r):
                for g in range(4):
                    ins = dve.tensor_scalar(dst[:, g, :], src[:, g, :], mv[:, g, 0:1], r[:, g:g + 1],
                                            ALU.subtract, ALU.mult)
                return ins

            def body(sa, sb_, sc):
                if sb_:
                    b = sb_
                    dve.wait_ge(cs_mm, b.n + 1)
                    dve.tensor_copy(hi4[:, :], ps[:, 6, 0:P]).then_inc(hi4_d, 1)
                    dve.wait_ge(hi4_d, b.n + 1)
                    dve.scalar_tensor_tensor(out=q[:, :], in0=hi4[:, :].bitcast(FP), scalar=negm[:, 0:1], in1=ps[:, 6, 0:P],
                                             op0=ALU.mult, op1=ALU.add).then_inc(q_d, 1)
                    dve.wait_ge(q_d, b.n + 1)
                    later(dve.wait_ge, d_mm, b.n * 4)
                    dve.tensor_tensor(rz[0:64], q[0:64, :].bitcast(FP).unsqueeze(1).to_broadcast([64, HEADS, P]),
                                      ind_h[0:64, :].unsqueeze(2).to_broadcast([64, HEADS, P]), ALU.mult).then_inc(rz_d, 1)
                    dve.tensor_tensor(l4[64:P], q[64:P, :].bitcast(FP).unsqueeze(1).to_broadcast([64, 4, P]),
                                      ind_g[64:P, :].unsqueeze(2).to_broadcast([64, 4, P]), ALU.mult).then_inc(l4_d, 1)
                if sa:
                    dve.wait_ge(zin_in[sa.s], sa.half * 16 + 16)
                    moments(zin[:, sa.s], st1, mv1, st1_d, mv1_d, sa.n)
                if sb_:
                    pair_dtx(sb_, 0)
                if sa:
                    dve.wait_ge(mv1_d, sa.n + 1)
                    dve.wait_ge(r1_p, sa.n + 1)
                    later(dve.wait_ge, ut_mm, sa.n)
                    norm(u, zin[:, sa.s], mv1, r1).then_inc(u_d, 1)
                if sb_:
                    weigh(sb_, 0)
                if sc:
                    n = sc.n
                    dve.wait_ge(o_mm, n + 1)
                    dve.wait_ge(zresb_p, n + 1)
                    dve.wait_ge(ry_p, n + 1)
                    later(dve.wait_ge, z2b_p, n)
                    for g in range(4):
                        ins = dve.scalar_tensor_tensor(out=z2[:, g, :], in0=ps[:, 2, g * P:(g + 1) * P],
                                                       scalar=ry[:, sc.s, g:g + 1], in1=zresb[:, g, :],
                                                       op0=ALU.mult, op1=ALU.add)
                    ins.then_inc(z2_d, 1)
                    dve.wait_ge(z2_d, n + 1)
                    moments(z2, st2, mv2, st2_d, mv2_d, n)
                if sb_:
                    weigh(sb_, 1)
                if sa:
                    dve.wait_ge(dt_mm, sa.n + 1)
                    dve.tensor_tensor(v[:, :].rearrange("p (g h) -> p g h", g=4),
                                      ps[:, 7, 0:HD].rearrange("p (g h) -> p g h", g=4),
                                      dtb[:, :].unsqueeze(1).to_broadcast([P, 4, HEADS]), ALU.add).then_inc(v_d, 1)
                    dve.wait_ge(v_d, sa.n + 1)
                    dve.scalar_tensor_tensor(out=vabs[:, :], in0=v[:, :], scalar=-1.0, in1=v[:, :],
                                             op0=ALU.mult, op1=ALU.max).then_inc(vabs_d, 1)
                    taps(sa, 0, 1)
                if sb_:
                    gate(sb_, 0)
                    weigh(sb_, 2)
                if sa:
                    dve.wait_ge(ve_a, sa.n + 1)
                    dve.tensor_scalar(vu[:, :], ve[:, :], 1.0, None, ALU.add).then_inc(vu_d, 1)
                if sb_:
                    pair_dtx(sb_, 1)
                if sc:
                    dve.wait_ge(mv2_d, sc.n + 1)
                    dve.wait_ge(r2_p, sc.n + 1)
                    norm(hn, z2, mv2, r2).then_inc(hn_d, 1)
                if sa:
                    taps(sa, 1, 2)
                if sb_:
                    gate(sb_, 1)
                    weigh(sb_, 3)
                if sa:
                    taps(sa, 2, 1)
                if sb_:
                    gate(sb_, 2)
                if sa:
                    n = sa.n
                    dve.wait_ge(vl_a, n + 1)
                    dve.wait_ge(vu_d, n + 1)
                    dve.scalar_tensor_tensor(out=vr[:, :], in0=vu[:, :], scalar=-1.0, in1=ve[:, :],
                                             op0=ALU.add, op1=ALU.subtract).then_inc(vr_d, 1)
                    dve.scalar_tensor_tensor(out=vx[:, :], in0=v[:, :], scalar=0.0, in1=vl[:, :],
                                             op0=ALU.max, op1=ALU.add).then_inc(vx_d, 1)
                    dve.wait_ge(vr_d, n + 1)
                    dve.wait_ge(vx_d, n + 1)
                    dve.tensor_tensor(dt[:, sa.s, :], vx[:, :], vr[:, :], ALU.subtract).then_inc(dt_d, 1)
                    dve.wait_ge(dt_d, n + 1)
                    dve.tensor_tensor(dta[:, sa.s], dt[:, sa.s, :].unsqueeze(1).to_broadcast([P, 4, HD]),
                                      amat[:, :].unsqueeze(1).to_broadcast([P, 4, HD]), ALU.mult).then_inc(dta_d, 1)
                if sb_:
                    gate(sb_, 3)
                if sc:
                    n = sc.n
                    dve.wait_ge(f2_mm, n + 1)
                    dve.wait_ge(z2b_p, n + 1)
                    later(dve.wait_ge, out_done[sc.s], sc.half * 16)
                    dve.tensor_tensor(outb[:, sc.s], four(ps[:, 2, :]), z2b[:, :, :], ALU.add).then_inc(fin_d, 1)

            pipeline(dve, QUADS, body)


def step_tables():
    import numpy as np
    p = np.arange(P)
    f = lambda m: np.ascontiguousarray(m, dtype=np.float32)
    sign = np.where(p < 64, 1.0, -1.0)[:, None]
    return {"tri": f(np.triu(np.ones((P, P)))),
            "ind_h": f(p[:, None] % HEADS == np.arange(HEADS)),
            "ind_g": f(sign * (p[:, None] % 32 // HEADS == np.arange(4))),
            "negm": f(-(p[:, None] // 32 % 2))}


def kernel(**inputs):
    import numpy as np
    import concourse.bacc as _bacc
    from concourse.bass_utils import run_bass_kernel_spmd as _run

    x = np.asarray(inputs["x"])
    arrays = {"x": x,
              "x_cols": x.transpose(0, 1, 3, 2).reshape(IMAGES, H, C // 4, 4 * W).transpose(0, 2, 1, 3)
                         .reshape(IMAGES * C // 4, H, 4 * W)}
    for n in ("w_h", "b_h", "w_l", "b_l", "b_f", "gamma", "beta"):
        arrays[n] = np.asarray(inputs["L0_conv_" + n])
    arrays["w_f"] = np.asarray(inputs["L0_conv_w_f"]).reshape(9, C, C)
    for n in ("ln1_w", "ln1_b", "ln2_w", "ln2_b", "conv_w", "dt_bias", "A_log", "out_proj_w",
              "ff_g", "ff_v", "ff_b", "fc1_g", "fc1_v", "fc1_b", "fc2_g", "fc2_v", "fc2_b"):
        arrays[n] = np.asarray(inputs["L1_conv_" + n])
    arrays["in_proj_t"] = np.asarray(inputs["L1_conv_in_proj_w"]).T
    arrays["conv_b3"] = np.asarray(inputs["L1_conv_conv_b"]).reshape(3, P).T
    arrays["d_cols"] = np.repeat(np.asarray(inputs["L1_conv_D_param"]), HEADDIM).reshape(2, P).T
    arrays["ssm_w2"] = np.asarray(inputs["L1_conv_ssm_norm_w"]).reshape(2, P).T
    arrays.update(dft_tables())
    arrays.update(step_tables())

    nc = _bacc.Bacc("TRN2", target_bir_lowering=False, num_devices=1)
    arrays = {"in_" + n: np.ascontiguousarray(v) for n, v in arrays.items()}
    a = {n[3:]: nc.dram_tensor(n, v.shape, FP, kind="ExternalInput").ap() for n, v in arrays.items()}
    z1 = nc.dram_tensor("z1", (IMAGES, H, W, C), FP, kind="Internal").ap()
    out = nc.dram_tensor("out", (QUADS, W, 4 * C), FP, kind="ExternalOutput").ap()
    spectral_block(nc, a, z1)
    sequence_block(nc, a, z1, out)
    r = _run(nc, [arrays], core_ids=[0])
    got = np.asarray(r.results[0]["out"])
    return got.reshape(IMAGES, H // 4, W, 4, C).transpose(0, 1, 3, 2, 4).reshape(IMAGES, H, W, C)
```

```python
from contextlib import ExitStack

import concourse.bass as bass
from concourse import mybir
from concourse.bass import ds

FP = mybir.dt.float32
FR = mybir.dt.float32r
BF = mybir.dt.bfloat16
ALU = mybir.AluOpType
ACT = mybir.ActivationFunctionType

P = 128
IMAGES, H, W, C = 4, 128, 128, 128
QUADS = IMAGES * H // 4
STRIP = H // 2
SROWS, SCOLS = STRIP + 2, W + 2
HALF = H // 2
HEADS, HEADDIM, DSTATE, DINNER = 8, 32, 64, 256
BIG = 1e30
EPS0, EPS1 = 1e-3, 1e-5
TINY = 1e-30
SBUF_START = 16640


class Place:

    def __init__(self, nc, tag, at=SBUF_START):
        self.nc, self.tag, self.at = nc, tag, at

    def __call__(self, name, shape, dt=FP):
        size = 2 if dt == BF else 4
        for n in shape[1:]:
            size *= n
        at = self.at
        self.at = (at + size + 63) // 64 * 64
        return self.nc.alloc_sbuf_tensor_at(self.tag + name, shape, dt, offset=at)


def eight_columns(sp, t, b, rows, g):
    return [t[ds(sp.snap(b), 1), rows, ds(sp.snap(g * 8 + 4 * e), 4), :].rearrange("o r w c -> (o r) (w c)")
            for e in range(2)]


def spectral_block(nc, a, z1):
    ctx = ExitStack()
    with ctx:
        def sem(name):
            return ctx.enter_context(nc.semaphore(name))

        def sems(name, n):
            return [sem(f"{name}{i}") for i in range(n)]

        sb = Place(nc, "f_")
        spec_at = sb.at
        spec = sb("spec", [P, 3 * HALF, C])
        rowspec = sb("rowspec", [P, P, C])
        work = sb("work", [P, 8, 512])
        xt = sb("xt", [P, 4, 512])
        edge = sb("edge", [P, 4, C])
        edge_amp = sb("edge_amp", [P, 2, C])
        dft_h, cosm, sinm, nsinm, ident, wh, wl, gamma, beta = (
            sb(n, [P, P]) for n in ("dft_h", "cosm", "sinm", "nsinm", "ident", "wh", "wl", "gamma", "beta"))
        idft_h = sb("idft_h", [P, H + 2])
        bias = sb("bias", [P, 3])
        wf_hi = sb("wf_hi", [P, 9, C], FR)
        wf_lo = sb("wf_lo", [P, 9, C], FR)
        stats = sb("stats", [P, 2, 4, 6])
        mv = sb("mv", [P, 2, 4, 2])
        rstd = sb("rstd", [P, 2, 4])
        mhalf = sb("mhalf", [P, 4])
        over = Place(nc, "f_", spec_at)
        s_hi = over("s_hi", [P, SCOLS, SROWS], FR)
        s_lo = over("s_lo", [P, SCOLS, SROWS], FR)
        conv_v = over("conv_v", [P, 2, 512])
        xres = over("xres", [P, 2, 512])
        ysum = over("ysum", [P, 2, 512])
        zout = over("zout", [P, 2, 512])
        wf_raw = over("wf_raw", [P, 9, C])

        ps = ctx.enter_context(nc.psum_tensor("f_ps", [P, 8, 512], FP))

        waited = sem("f_waited")
        consts_in, wf_in = sem("f_consts_in"), sem("f_wf_in")
        wf_hi_ready, wf_ready, mhalf_ready = sem("f_wf_hi_ready"), sem("f_wf_ready"), sem("f_mhalf_ready")
        x_in, y_mm, y_free = sems("f_x_in", 4), sems("f_y_mm", 4), sems("f_y_free", 4)
        f_mm, re_ready, im_ready, im_sq, ss_ready, amp_ready = (
            sems("f_" + n, 2) for n in ("f_mm", "re_ready", "im_ready", "im_sq", "ss_ready", "amp_ready"))
        edge_mm, edge_copied, edge_sq, edge_ss, edge_amp_ready = (
            sem("f_" + n) for n in ("edge_mm", "edge_copied", "edge_sq", "edge_ss", "edge_amp_ready"))
        ampT_mm, ampT_ready, gate_mm, sig_ready, gsum_ready, gT_mm, gated, neg_done, edge_scaled = (
            sem("f_" + n) for n in ("ampT_mm", "ampT_ready", "gate_mm", "sig_ready", "gsum_ready",
                                    "gT_mm", "gated", "neg_done", "edge_scaled"))
        t_mm, t_free = sem("f_t_mm"), sems("f_t_free", 4)
        s_mm, hi_ready, lo_ready, pad_ready = (sem("f_" + n) for n in ("s_mm", "hi_ready", "lo_ready", "pad_ready"))
        conv_mm, silu_done, vT_mm, ysum_done, stats_done, mv_ready, var_eps, rstd_ready, scaled, z_ready = (
            sems("f_" + n, 2) for n in ("conv_mm", "silu_done", "vT_mm", "ysum_done", "stats_done",
                                        "mv_ready", "var_eps", "rstd_ready", "scaled", "z_ready"))
        xres_in, z_out = sems("f_xres_in", 2), sems("f_z_out", 2)

        GROUPS = HALF // 4
        G17 = GROUPS + 1
        NCONST = 16 * 13

        block = ctx.enter_context(nc.Block())

        @block.sync
        def _(sp):
            for one in z_out:
                sp.sem_inc(one)
            for t, src in ((dft_h, a["dft_h"]), (cosm, a["cosm"]), (sinm, a["sinm"]), (nsinm, a["nsinm"]),
                           (ident, a["ident"]), (wh, a["w_h"]), (wl, a["w_l"]), (idft_h, a["idft_h"])):
                sp.dma_start(t[:, :], src).then_inc(consts_in, 16)
            for n, src in enumerate((a["b_h"], a["b_l"], a["b_f"])):
                sp.dma_start(bias[:, n:n + 1], src.rearrange("(p o) -> p o", o=1)).then_inc(consts_in, 16)
            sp.dma_start(gamma[:, :], a["gamma"].partition_broadcast(P)).then_inc(consts_in, 16)
            sp.dma_start(beta[:, :], a["beta"].partition_broadcast(P)).then_inc(consts_in, 16)
            sp.dma_start(wf_raw[:, :, :], a["w_f"].rearrange("t c d -> c t d")).then_inc(wf_in, 16)
            def x_tile(t):
                for j in range(4):
                    src = a["x_cols"][ds(sp.snap(t * 4 + j), 1)].rearrange("o h n -> h (o n)")
                    free = sp.snap(t + 1)
                    sp.wait_ge(y_mm[j], free)
                    sp.dma_start(xt[:, j, :], src).then_inc(x_in[j], 16)

            def image(b, last):
                with sp.Fori(0, 7) as t:
                    x_tile(b * 8 + t + 1)
                done = sp.snap(b * 32 + 32)
                sp.wait_ge(t_mm, done)
                sp.sem_inc(waited)
                for strip in range(2):
                    if strip == 1 and not last:
                        x_tile(b * 8 + 8)
                    rows = slice(strip * STRIP, (strip + 1) * STRIP)
                    for s in range(2):
                        srcs = eight_columns(sp, a["x"], b, rows, s)
                        use = sp.snap(b * 16 + (strip * 8 + 1))
                        sp.wait_ge(ysum_done[s], use)
                        for e in range(2):
                            sp.dma_start(xres[e * STRIP:(e + 1) * STRIP, s, :], srcs[e]).then_inc(xres_in[s], 16)
                    with sp.Fori(0, 7) as j:
                        for s in range(2):
                            srcs = eight_columns(sp, a["x"], b, rows, j * 2 + (s + 2))
                            dsts = eight_columns(sp, z1, b, rows, j * 2 + s)
                            use = sp.snap(b * 16 + (strip * 8 + 1) + j)
                            added = sp.snap(b * 16 + (strip * 8 + 2) + j)
                            sp.wait_ge(ysum_done[s], added)
                            for e in range(2):
                                sp.dma_start(xres[e * STRIP:(e + 1) * STRIP, s, :], srcs[e]).then_inc(xres_in[s], 16)
                            sp.wait_ge(z_ready[s], use)
                            for e in range(2):
                                sp.dma_start(dsts[e], zout[e * STRIP:(e + 1) * STRIP, s, :]).then_inc(z_out[s], 16)
                    for s in range(2):
                        dsts = eight_columns(sp, z1, b, rows, 14 + s)
                        use = sp.snap(b * 16 + (strip * 8 + 8))
                        sp.wait_ge(z_ready[s], use)
                        for e in range(2):
                            sp.dma_start(dsts[e], zout[e * STRIP:(e + 1) * STRIP, s, :]).then_inc(z_out[s], 16)
            x_tile(0)
            with sp.Fori(0, IMAGES - 1) as b:
                image(b, False)
            image(IMAGES - 1, True)
            for s in range(2):
                sp.wait_ge(z_out[s], 32 * IMAGES * 16 + 1)

        @block.tensor
        def _(pe):
            def conv(use, r, s):
                pe.wait_ge(silu_done[s], use + 1)
                for tap in range(9):
                    ky, kx = tap // 3, tap % 3
                    hi = s_hi[:, ds(r * 8 + kx, 8), ky:ky + STRIP]
                    lo = s_lo[:, ds(r * 8 + kx, 8), ky:ky + STRIP]
                    out = ps[:, 4 + s, :].rearrange("p (w r) -> p w r", w=8)
                    pe.matmul(out, wf_hi[:, tap, :], hi, start=(tap == 0), stop=False)
                    pe.matmul(out, wf_hi[:, tap, :], lo, start=False, stop=False)
                    mm = pe.matmul(out, wf_lo[:, tap, :], hi, start=False, stop=(tap == 8))
                mm.then_inc(conv_mm[s], 1)

            def turn(use, s):
                pe.wait_ge(silu_done[s], use + 2)
                pe.wait_ge(ysum_done[s], use + 1)
                for k in range(4):
                    mm = pe.transpose(ps[:, 6 + s, k * P:(k + 1) * P], conv_v[:, s, k * P:(k + 1) * P], ident[:, :])
                mm.then_inc(vT_mm[s], 1)

            pe.wait_ge(consts_in, NCONST)
            pe.wait_ge(wf_ready, 1)
            for one in (*y_mm, *vT_mm):
                pe.sem_inc(one)
            with pe.Fori(0, IMAGES) as b:
                with pe.Fori(0, 8) as t:
                    for j in range(4):
                        pe.wait_ge(x_in[j], b * 128 + t * 16 + 16)
                        pe.wait_ge(y_free[j], b * 8 + t + 1)
                        for c in range(4):
                            mm = pe.matmul(ps[:, j, c * P:(c + 1) * P], xt[:, j, c * P:(c + 1) * P], dft_h[:, :],
                                           start=True, stop=True)
                        mm.then_inc(y_mm[j], 1)
                for j in range(4):
                    pe.wait_ge(y_free[j], b * 8 + 9)
                pe.sem_inc(waited)
                with pe.Fori(0, GROUPS // 2) as q:
                    for s in range(2):
                        pe.wait_ge(re_ready[s], b * 8 + q + 1)
                        pe.wait_ge(im_ready[s], b * 8 + q + 1)
                        y_re = rowspec[:, ds(q * 8 + s * 4, 4), :]
                        y_im = rowspec[:, ds(q * 8 + s * 4 + HALF, 4), :]
                        out_re = ps[:, 2 * s, :].rearrange("p (r c) -> p r c", r=4)
                        out_im = ps[:, 2 * s + 1, :].rearrange("p (r c) -> p r c", r=4)
                        pe.matmul(out_re, cosm[:, :], y_re, start=True, stop=False)
                        pe.matmul(out_im, cosm[:, :], y_im, start=True, stop=False)
                        pe.matmul(out_re, sinm[:, :], y_im, start=False, stop=True)
                        pe.matmul(out_im, nsinm[:, :], y_re, start=False, stop=True).then_inc(f_mm[s], 1)
                for s in range(2):
                    pe.wait_ge(silu_done[s], b * 16 + 1)
                    pe.wait_ge(ysum_done[s], b * 16 + 1)
                for n, (w, row) in enumerate(((cosm, 0), (nsinm, 0), (sinm, HALF), (cosm, HALF))):
                    mm = pe.matmul(ps[:, 4, n * P:(n + 1) * P], w[:, :], rowspec[:, row, :], start=True, stop=True)
                mm.then_inc(edge_mm, 1)
                for s in range(2):
                    pe.wait_ge(amp_ready[s], b * 8 + 9)
                    pe.wait_ge(re_ready[s], b * 8 + 9)
                    pe.wait_ge(im_ready[s], b * 8 + 9)
                for q in range(G17 + 2):
                    if q < G17:
                        if q >= 2:
                            pe.wait_ge(ampT_ready, b * G17 + (q - 1))
                        if q == GROUPS:
                            pe.wait_ge(edge_amp_ready, b + 1)
                        for k in range(4 if q < GROUPS else 2):
                            src = spec[:, 4 * q + k, :] if q < GROUPS else edge_amp[:, k, :]
                            mm = pe.transpose(ps[:, q % 2, k * P:(k + 1) * P], src, ident[:, :])
                        mm.then_inc(ampT_mm, 1)
                    if 1 <= q <= G17:
                        g = q - 1
                        n = 512 if g < GROUPS else 256
                        pe.wait_ge(ampT_ready, b * G17 + (g + 1))
                        if g >= 2:
                            pe.wait_ge(sig_ready, b * G17 + (g - 1))
                        if g == 1:
                            pe.wait_ge(edge_copied, b + 1)
                            pe.wait_ge(edge_sq, b + 1)
                        for w, bank in ((wh, 2), (wl, 3)):
                            mm = pe.matmul(ps[:, bank + 2 * (g % 2), 0:n], w[:, :], work[:, g % 2, 0:n],
                                           start=True, stop=True)
                        mm.then_inc(gate_mm, 1)
                    if q >= 2:
                        g = q - 2
                        pe.wait_ge(gsum_ready, b * G17 + (g + 1))
                        if g >= 2:
                            pe.wait_ge(gated, b * G17 + (g - 1))
                        for k in range(4 if g < GROUPS else 2):
                            mm = pe.transpose(ps[:, 6 + g % 2, k * P:(k + 1) * P],
                                              work[:, 6 + g % 2, k * P:(k + 1) * P], ident[:, :])
                        mm.then_inc(gT_mm, 1)
                pe.wait_ge(gated, b * G17 + G17)
                pe.wait_ge(neg_done, b * G17 + G17)
                for j in range(C // 4):
                    if j >= 4:
                        pe.wait_ge(t_free[j % 4], b * 8 + j // 4)
                    for k in range(4):
                        out = ps[:, j % 4, k * P:(k + 1) * P]
                        pe.matmul(out, spec[:, HALF:3 * HALF, 4 * j + k], cosm[:, :], start=True, stop=False)
                        mm = pe.matmul(out, spec[:, 0:2 * HALF, 4 * j + k], sinm[:, :], start=False, stop=True)
                    mm.then_inc(t_mm, 1)
                for j in range(4):
                    pe.wait_ge(t_free[j], b * 8 + 8)
                for strip in range(2):
                    for j in range(W // 8):
                        if j >= 2:
                            pe.wait_ge(lo_ready, b * 32 + (strip * 16 + j - 1))
                        for k in range(8):
                            mm = pe.matmul(ps[:, 2 * (j % 2) + k // 4, (k % 4) * SROWS:(k % 4 + 1) * SROWS],
                                           rowspec[:, :, 8 * j + k], idft_h[:, strip * STRIP:strip * STRIP + SROWS],
                                           start=True, stop=True)
                        mm.then_inc(s_mm, 1)
                    pe.wait_ge(lo_ready, b * 32 + (strip * 16 + 16))
                    pe.wait_ge(pad_ready, b * 2 + 2)
                    use = b * 16 + strip * 8
                    conv(use, 0, 0)
                    with pe.Fori(0, 7) as j:
                        conv(b * 16 + strip * 8 + j, j * 2 + 1, 1)
                        turn(b * 16 + strip * 8 + j, 0)
                        conv(b * 16 + (strip * 8 + 1) + j, j * 2 + 2, 0)
                        turn(b * 16 + strip * 8 + j, 1)
                    conv(b * 16 + (strip * 8 + 7), 15, 1)
                    turn(b * 16 + (strip * 8 + 7), 0)
                    turn(b * 16 + (strip * 8 + 7), 1)

        @block.scalar
        def _(act):
            act.wait_ge(consts_in, NCONST)
            act.wait_ge(wf_in, 16)
            act.activation(wf_hi[:, :, :], wf_raw[:, :, :], ACT.Copy).then_inc(wf_hi_ready, 1)
            for one in (y_free[0], y_free[2], *re_ready, *amp_ready, *silu_done):
                act.sem_inc(one)
            with act.Fori(0, IMAGES) as b:
                with act.Fori(0, 8) as t:
                    for j in (0, 2):
                        act.wait_ge(y_mm[j], b * 8 + t + 2)
                        act.activation(rowspec[:, :, ds(t * 16 + 4 * j, 4)].rearrange("p k c -> p c k"),
                                       ps[:, j, :].rearrange("p (c k) -> p c k", c=4), ACT.Copy).then_inc(y_free[j], 1)
                act.preload_act_table(ACT.Sqrt)
                with act.Fori(0, GROUPS // 2) as q:
                    for s in range(2):
                        act.wait_ge(f_mm[s], b * 8 + q + 1)
                        act.activation(spec[:, ds(q * 8 + s * 4 + HALF, 4), :],
                                       ps[:, 2 * s, :].rearrange("p (r c) -> p r c", r=4), ACT.Copy)
                        act.activation(work[:, 2 * s, :], ps[:, 2 * s, :], ACT.Square).then_inc(re_ready[s], 1)
                        act.wait_ge(ss_ready[s], b * 8 + q + 1)
                        act.activation(spec[:, ds(q * 8 + s * 4, 4), :],
                                       work[:, 4 + s, :].rearrange("p (r c) -> p r c", r=4),
                                       ACT.Sqrt).then_inc(amp_ready[s], 1)
                act.wait_ge(edge_mm, b + 1)
                act.activation(work[:, 6, :], ps[:, 4, :], ACT.Square).then_inc(edge_sq, 1)
                act.wait_ge(edge_ss, b + 1)
                act.activation(edge_amp[:, :, :], work[:, 7, 0:256].rearrange("p (r c) -> p r c", r=2),
                               ACT.Sqrt).then_inc(edge_amp_ready, 1)
                for g in range(G17):
                    n = 512 if g < GROUPS else 256
                    act.wait_ge(gate_mm, b * G17 + (g + 1))
                    if g >= 2:
                        act.wait_ge(gsum_ready, b * G17 + (g - 1))
                    for k in range(2):
                        ins = act.activation(work[:, 2 + 2 * (g % 2) + k, 0:n], ps[:, 2 + 2 * (g % 2) + k, 0:n],
                                             ACT.Sigmoid, bias=bias[:, k:k + 1])
                    ins.then_inc(sig_ready, 1)
                for j in range(0, C // 4, 2):
                    act.wait_ge(t_mm, b * 32 + (j + 1))
                    act.activation(rowspec[:, 4 * j:4 * j + 4, :],
                                   ps[:, j % 4, :].rearrange("p (c w) -> p c w", c=4), ACT.Copy).then_inc(t_free[j % 4], 1)
                for strip in range(2):
                    for j in range(W // 8):
                        act.wait_ge(s_mm, b * 32 + (strip * 16 + j + 1))
                        act.activation(s_hi[:, 1 + 8 * j:9 + 8 * j, :].rearrange("p (b w) r -> p b w r", b=2),
                                       ps[:, 2 * (j % 2):2 * (j % 2) + 2, 0:4 * SROWS]
                                       .rearrange("p b (w r) -> p b w r", r=SROWS), ACT.Copy).then_inc(hi_ready, 1)
                    act.preload_act_table(ACT.Silu)
                    with act.Fori(0, 8) as j:
                        for s in range(2):
                            act.wait_ge(conv_mm[s], b * 16 + (strip * 8 + 1) + j)
                            act.wait_ge(vT_mm[s], b * 16 + strip * 8 + j + 1)
                            act.activation(conv_v[:, s, :].rearrange("p (k e r) -> p e k r", k=4, e=2),
                                           ps[:, 4 + s, :].rearrange("p (e k r) -> p e k r", k=4, e=2), ACT.Silu,
                                           bias=bias[:, 2:3]).then_inc(silu_done[s], 1)

        @block.vector
        def _(dve):
            def rest(b, strip, j):
                dve.wait_ge(hi_ready, b * 32 + (strip * 16 + j + 1))
                cols = (slice(None), slice(1 + 8 * j, 9 + 8 * j), slice(None))
                dve.tensor_tensor(s_lo[cols].rearrange("p (b w) r -> p b w r", b=2),
                                  ps[:, 2 * (j % 2):2 * (j % 2) + 2, 0:4 * SROWS]
                                  .rearrange("p b (w r) -> p b w r", r=SROWS),
                                  s_hi[cols].bitcast(FP).rearrange("p (b w) r -> p b w r", b=2),
                                  ALU.subtract).then_inc(lo_ready, 1)

            def residual(use, s, loaded):
                dve.wait_ge(vT_mm[s], use + 2)
                dve.wait_ge(xres_in[s], loaded)
                dve.tensor_tensor(ysum[:, s, :], ps[:, 6 + s, :], xres[:, s, :], ALU.add).then_inc(ysum_done[s], 1)

            def moments(use, s):
                dve.wait_ge(ysum_done[s], use + 2)
                for r in range(4):
                    ins = dve.bn_stats(stats[:, s, r, :], ysum[:, s, r * P:(r + 1) * P])
                ins.then_inc(stats_done[s], 1)
                dve.wait_ge(stats_done[s], use + 1)
                dve.sem_inc(waited)
                for r in range(4):
                    ins = dve.bn_aggr(mv[:, s, r, :], stats[:, s, r, :])
                ins.then_inc(mv_ready[s], 1)

            def scale(use, s, stored):
                dve.wait_ge(mv_ready[s], use + 1)
                dve.wait_ge(z_out[s], stored)
                for r in range(4):
                    ins = dve.scalar_tensor_tensor(out=zout[:, s, r * P:(r + 1) * P], in0=ysum[:, s, r * P:(r + 1) * P],
                                                   scalar=mv[:, s, r, 0:1], in1=gamma[:, :],
                                                   op0=ALU.subtract, op1=ALU.mult)
                ins.then_inc(scaled[s], 1)

            def shift(use, s):
                dve.wait_ge(scaled[s], use + 1)
                dve.wait_ge(rstd_ready[s], use + 1)
                for r in range(4):
                    ins = dve.scalar_tensor_tensor(out=zout[:, s, r * P:(r + 1) * P], in0=zout[:, s, r * P:(r + 1) * P],
                                                   scalar=rstd[:, s, r:r + 1], in1=beta[:, :],
                                                   op0=ALU.mult, op1=ALU.add)
                ins.then_inc(z_ready[s], 1)

            dve.wait_ge(consts_in, NCONST)
            dve.wait_ge(wf_hi_ready, 1)
            dve.tensor_tensor(wf_lo[:, :, :], wf_raw[:, :, :], wf_hi[:, :, :].bitcast(FP), ALU.subtract).then_inc(wf_ready, 1)
            for one in (y_free[1], y_free[3], *im_ready, *ysum_done):
                dve.sem_inc(one)
            with dve.Fori(0, IMAGES) as b:
                with dve.Fori(0, 8) as t:
                    for j in (1, 3):
                        dve.wait_ge(y_mm[j], b * 8 + t + 2)
                        dve.tensor_copy(rowspec[:, :, ds(t * 16 + 4 * j, 4)].rearrange("p k c -> p c k"),
                                        ps[:, j, :].rearrange("p (c k) -> p c k", c=4)).then_inc(y_free[j], 1)
                for s in range(2):
                    dve.wait_ge(z_out[s], b * 512 + 1)
                dve.sem_inc(waited)
                with dve.Fori(0, GROUPS // 2) as q:
                    for s in range(2):
                        dve.wait_ge(f_mm[s], b * 8 + q + 1)
                        im = spec[:, ds(q * 8 + s * 4 + 2 * HALF, 4), :]
                        dve.tensor_copy(im, ps[:, 2 * s + 1, :].rearrange("p (r c) -> p r c", r=4)).then_inc(im_ready[s], 1)
                        dve.wait_ge(im_ready[s], b * 8 + q + 2)
                        dve.tensor_tensor(work[:, 2 * s + 1, :].rearrange("p (r c) -> p r c", r=4), im, im,
                                          ALU.mult).then_inc(im_sq[s], 1)
                        dve.wait_ge(im_sq[s], b * 8 + q + 1)
                        dve.wait_ge(re_ready[s], b * 8 + q + 2)
                        dve.wait_ge(amp_ready[s], b * 8 + q + 1)
                        dve.scalar_tensor_tensor(out=work[:, 4 + s, :], in0=work[:, 2 * s, :], scalar=TINY,
                                                 in1=work[:, 2 * s + 1, :], op0=ALU.max, op1=ALU.add).then_inc(ss_ready[s], 1)
                dve.wait_ge(edge_sq, b + 1)
                dve.tensor_copy(edge[:, :, :], ps[:, 4, :].rearrange("p (r c) -> p r c", r=4)).then_inc(edge_copied, 1)
                pairs = work[:, 6, :].rearrange("p (k r c) -> p k r c", k=2, r=2)
                dve.scalar_tensor_tensor(out=work[:, 7, 0:256].rearrange("p (k c) -> p k c", k=2), in0=pairs[:, :, 0, :],
                                         scalar=TINY, in1=pairs[:, :, 1, :], op0=ALU.max, op1=ALU.add).then_inc(edge_ss, 1)
                for q in range(G17 + 2):
                    if q < G17:
                        n = 512 if q < GROUPS else 256
                        dve.wait_ge(ampT_mm, b * G17 + (q + 1))
                        if q >= 2:
                            dve.wait_ge(gate_mm, b * G17 + (q - 1))
                        dve.tensor_copy(work[:, q % 2, 0:n], ps[:, q % 2, 0:n]).then_inc(ampT_ready, 1)
                    if 1 <= q <= G17:
                        g = q - 1
                        n = 512 if g < GROUPS else 256
                        dve.wait_ge(sig_ready, b * G17 + (g + 1))
                        if g >= 2:
                            dve.wait_ge(gT_mm, b * G17 + (g - 1))
                        dve.tensor_tensor(work[:, 6 + g % 2, 0:n], work[:, 2 + 2 * (g % 2), 0:n],
                                          work[:, 3 + 2 * (g % 2), 0:n], ALU.add).then_inc(gsum_ready, 1)
                    if q >= 2:
                        g = q - 2
                        dve.wait_ge(gT_mm, b * G17 + (g + 1))
                        gate = ps[:, 6 + g % 2, :].rearrange("p (r c) -> p r c", r=4)
                        if g < GROUPS:
                            for row in (HALF + 4 * g, 2 * HALF + 4 * g):
                                part = spec[:, row:row + 4, :]
                                ins = dve.tensor_tensor(part, part, gate, ALU.mult)
                            ins.then_inc(gated, 1)
                        else:
                            for k in range(2):
                                part = edge[:, 2 * k:2 * k + 2, :]
                                ins = dve.tensor_tensor(part, part, gate[:, k:k + 1, :].to_broadcast([P, 2, C]), ALU.mult)
                            ins.then_inc(edge_scaled, 1)
                            dve.wait_ge(edge_scaled, b + 1)
                            dve.tensor_tensor(spec[:, HALF:3 * HALF:HALF, :], edge[:, 0:2, :], edge[:, 2:4, :],
                                              ALU.add).then_inc(gated, 1)
                for j in range(1, C // 4, 2):
                    dve.wait_ge(t_mm, b * 32 + (j + 1))
                    dve.tensor_copy(rowspec[:, 4 * j:4 * j + 4, :],
                                    ps[:, j % 4, :].rearrange("p (c w) -> p c w", c=4)).then_inc(t_free[j % 4], 1)
                for strip in range(2):
                    for j in range(6 if strip else 0, W // 8):
                        rest(b, strip, j)
                    with dve.Fori(0, 7) as j:
                        for s in range(2):
                            use = b * 16 + strip * 8 + j
                            residual(use, s, b * 512 + (strip * 256 + 32) + j * 32)
                            moments(use, s)
                            scale(use, s, b * 512 + (strip * 256 + 1) + j * 32)
                            shift(use, s)
                    use = b * 16 + (strip * 8 + 7)
                    for s in range(2):
                        residual(use, s, b * 512 + (strip * 256 + 256))
                    for s in range(2):
                        if strip == 0:
                            rest(b, 1, 3 * s)
                        moments(use, s)
                        if strip == 0:
                            rest(b, 1, 3 * s + 1)
                        scale(use, s, b * 512 + (strip * 256 + 225))
                        if strip == 0:
                            rest(b, 1, 3 * s + 2)
                        shift(use, s)

        @block.gpsimd
        def _(pool):
            pool.memset(mhalf[:, :], -0.5).then_inc(mhalf_ready, 1)
            pool.wait_ge(mhalf_ready, 1)
            with pool.Fori(0, IMAGES) as b:
                for g in range(G17):
                    pool.wait_ge(gated, b * G17 + (g + 1))
                    pool.sem_inc(waited)
                    first, last = (max(4 * g, 1), 4 * g + 4) if g < GROUPS else (0, 1)
                    pool.tensor_scalar(spec[:, first:last, :], spec[:, 2 * HALF + first:2 * HALF + last, :], -1.0, 1.0,
                                       ALU.mult, ALU.mult).then_inc(neg_done, 1)
                pool.wait_ge(t_mm, b * 32 + 32)
                pool.sem_inc(waited)
                for t in (s_hi, s_lo):
                    pool.memset(t[:, 0:SCOLS:SCOLS - 1, :].bitcast(FP), 0.0).then_inc(pad_ready, 1)
                for strip in range(2):
                    with pool.Fori(0, 8) as j:
                        for s in range(2):
                            use = b * 16 + strip * 8 + j
                            pool.wait_ge(mv_ready[s], use + 1)
                            pool.sem_inc(waited)
                            pool.tensor_scalar(rstd[:, s, :], mv[:, s, :, 1], EPS0, None, ALU.add).then_inc(var_eps[s], 1)
                            pool.wait_ge(var_eps[s], use + 1)
                            pool.tensor_tensor(rstd[:, s, :], rstd[:, s, :], mhalf[:, :], ALU.pow).then_inc(rstd_ready[s], 1)


def dft_tables():
    import numpy as np
    n = np.arange(P)
    angle = 2 * np.pi * np.outer(n, n) / P
    cos, sin = (np.where(abs(m) < 1e-9, 0.0, m) for m in (np.cos(angle), np.sin(angle)))
    alt = (-1.0) ** n
    dft_h = np.concatenate([cos[:, :HALF], alt[:, None], -sin[:, 1:HALF]], axis=1)
    inv = np.zeros((P, H + 2))
    scale = 1.0 / (H * W)
    inv[0, 1:H + 1] = scale
    inv[1:HALF, 1:H + 1] = 2 * scale * cos[1:HALF]
    inv[HALF, 1:H + 1] = scale * alt
    inv[HALF + 1:, 1:H + 1] = -2 * scale * sin[1:HALF]
    f = lambda m: np.ascontiguousarray(m, dtype=np.float32)
    return {"dft_h": f(dft_h), "cosm": f(cos), "sinm": f(sin), "nsinm": f(-sin), "idft_h": f(inv),
            "ident": f(np.eye(P))}


class Step:

    def __init__(self, n, half, parity):
        self.n, self.half, self.s = n, half, parity


def pipeline(engine, steps, body):
    head = 4

    def at(n):
        return Step(n, n // 2, n % 2) if 0 <= n < steps else None

    for n in range(-1, head):
        body(at(n + 1), at(n), at(n - 1), at(n - 2))
    with engine.Fori(head // 2, steps // 2 - 1) as m:
        for s in range(2):
            body(Step(m * 2 + (s + 1), m + s, 1 - s), Step(m * 2 + s, m, s),
                 Step(m * 2 + (s - 1), m + (s - 1), 1 - s), Step(m * 2 + (s - 2), m - 1, s))
    for n in range(steps - 2, steps + 3):
        body(at(n + 1), at(n), at(n - 1), at(n - 2))


def later(wait, sem, value):
    if not isinstance(value, int) or value > 0:
        wait(sem, value)


def four(t):
    return t.rearrange("p (g n) -> p g n", g=4)


def sequence_block(nc, a, z1, out):
    ctx = ExitStack()
    with ctx:
        def sem(name):
            return ctx.enter_context(nc.semaphore("g_" + name))

        def sems(name, n):
            return [sem(f"{name}{i}") for i in range(n)]

        HD = 4 * HEADS
        sb = Place(nc, "g_")
        ident, tri = sb("ident", [P, P]), sb("tri", [P, P])
        ident_b, mask_b = sb("ident_b", [P, P], BF), sb("mask_b", [P, P], BF)
        wx, wz, wdt = sb("wx", [P, 3 * P]), sb("wz", [P, 2 * P]), sb("wdt", [P, HEADS])
        conv_w, conv_b = sb("conv_w", [P, 3, 4]), sb("conv_b", [P, 3])
        lncol = sb("lncol", [P, 4])
        fc1_b = sb("fc1_b", [P, 1])
        dtb, alog, aexp = sb("dtb", [P, HEADS]), sb("alog", [P, HEADS]), sb("aexp", [P, HEADS])
        amat = sb("amat", [P, HD])
        dcol, diag = sb("dcol", [P, 2]), sb("diag", [P, 2, P])
        ssm_w, op_raw = sb("ssm_w", [P, 2]), sb("op_raw", [P, DINNER])
        vraw, gcol, vsq = sb("vraw", [P, 3, P]), sb("gcol", [P, 3]), sb("vsq", [P, 3])
        vn, wt = sb("vn", [P, 3, P]), sb("wt", [P, 3, P])
        wc = sb("wc", [P, 2, P])
        ffb, fc2b = sb("ffb", [P, P]), sb("fc2b", [P, P])
        mhalf = sb("mhalf", [P, HD])
        ind_h, ind_g, negm = sb("ind_h", [P, HEADS]), sb("ind_g", [P, 4]), sb("negm", [P, 1])
        zin, zres, outb = (sb(n, [P, 2, 4, P]) for n in ("zin", "zres", "outb"))
        zresb, u, z2, z2b, hn = (sb(n, [P, 4, P]) for n in ("zresb", "u", "z2", "z2b", "hn"))
        ut, ht, gl = (sb(n, [P, 4 * P]) for n in ("ut", "ht", "gl"))
        acc = sb("acc", [P, 3, 4, P])
        tap1 = sb("tap1", [P, 2, 4, P])
        xs = sb("xs", [P, 2, 2, 4, P])
        bmat, cmat = sb("bmat", [DSTATE, 2, 4, P]), sb("cmat", [DSTATE, 2, 4, P])
        zs, yg = sb("zs", [P, 2, 4, DINNER]), sb("yg", [P, 2, 4, DINNER])
        v, vabs, ve, vu, vl, vr, vx = (sb(n, [P, HD]) for n in ("v", "vabs", "ve", "vu", "vl", "vr", "vx"))
        dt, dta = sb("dt", [P, 2, HD]), sb("dta", [P, 2, 4, HD])
        hi4, q = sb("hi4", [P, P], FR), sb("q", [P, P], FR)
        rz, l4 = sb("rz", [P, HEADS, P], FR), sb("l4", [P, 4, P], FR)
        emat, mmat = sb("emat", [P, 2, 8 * P]), sb("mmat", [P, 2, 8 * P])
        dtx = sb("dtx", [P, 2, 512])
        ygt = sb("ygt", [P, 4, 2, P])
        junk = sb("junk", [P, DINNER])
        ss, ry = sb("ss", [P, 2, 4]), sb("ry", [P, 2, 4])
        st1, st2, mv1, mv2 = sb("st1", [P, 4, 6]), sb("st2", [P, 4, 6]), sb("mv1", [P, 4, 2]), sb("mv2", [P, 4, 2])
        r1, r2 = sb("r1", [P, 4]), sb("r2", [P, 4])

        ps = ctx.enter_context(nc.psum_tensor("g_ps", [P, 8, 512], FP))

        waited = sem("waited")
        TAPS_A, TAPS_D = 5, 7
        add_p = sem("add_p")
        win = sem("win")
        const_p, const_d, const_a = sem("const_p"), sem("const_d"), sem("const_a")
        a_ready, vsq_ready, vrs_ready, vn_ready, wt_mm, wt_ready, wc_mm, wc_ready = (
            sem(n) for n in ("a_ready", "vsq_ready", "vrs_ready", "vn_ready", "wt_mm", "wt_ready", "wc_mm", "wc_ready"))
        zin_in, zres_in, out_done = sems("zin_in", 2), sems("zres_in", 2), sems("out_done", 2)
        zresb_p, z2b_p, r1a_p, r1_p, r2a_p, r2_p, rya_p, ry_p = (
            sem(n) for n in ("zresb_p", "z2b_p", "r1a_p", "r1_p", "r2a_p", "r2_p", "rya_p", "ry_p"))
        ygt_mm, d_mm, xt_mm, y_mm, x_mm, z_mm, cs_mm, cb_mm, ut_mm, o_mm, dt_mm, ht_mm, f1_mm, f2_mm = (
            sem(n) for n in ("ygt_mm", "d_mm", "xt_mm", "y_mm", "x_mm", "z_mm", "cs_mm", "cb_mm", "ut_mm", "o_mm",
                             "dt_mm", "ht_mm", "f1_mm", "f2_mm"))
        ut_a, e_a, tap_a, sq_a, ve_a, vl_a, ht_a, gl_a, xs_a, bc_a, zs_a = (
            sem(n) for n in ("ut_a", "e_a", "tap_a", "sq_a", "ve_a", "vl_a", "ht_a", "gl_a", "xs_a", "bc_a", "zs_a"))
        hi4_d, q_d, rz_d, l4_p, st1_d, mv1_d, dtx_d, u_p, m_d, z2_d, st2_d, mv2_d = (
            sem(n) for n in ("hi4_d", "q_d", "rz_d", "l4_p", "st1_d", "mv1_d", "dtx_d", "u_p", "m_d", "z2_d", "st2_d",
                             "mv2_d"))
        v_d, vabs_d, ygt_d, conv_d, gate_d, vu_d, hn_d, vr_d, vx_d, dt_d, dta_d, fin_d = (
            sem(n) for n in ("v_d", "vabs_d", "ygt_d", "conv_d", "gate_d", "vu_d", "hn_d", "vr_d", "vx_d", "dt_d", "dta_d", "fin_d"))

        def col(src):
            return src.rearrange("(p o) -> p o", o=1)

        loads = [(ident[:, :], a["ident"]), (tri[:, :], a["tri"]), (wx[:, :], a["in_proj_t"][:, 256:640]),
                 (wz[:, :], a["in_proj_t"][:, 0:256]), (wdt[:, :], a["in_proj_t"][:, 640:648]),
                 (conv_w[:, :, :], a["conv_w"].rearrange("(j p) k -> p j k", j=3)), (conv_b[:, :], a["conv_b3"]),
                 (dcol[:, :], a["d_cols"]), (ssm_w[:, :], a["ssm_w2"]),
                 (lncol[:, 0:1], col(a["ln1_w"])), (lncol[:, 1:2], col(a["ln1_b"])),
                 (lncol[:, 2:3], col(a["ln2_w"])), (lncol[:, 3:4], col(a["ln2_b"])), (fc1_b[:, :], col(a["fc1_b"])),
                 (dtb[:, :], a["dt_bias"].partition_broadcast(P)), (alog[:, :], a["A_log"].partition_broadcast(P)),
                 (op_raw[:, :], a["out_proj_w"]), (vraw[:, 0, :], a["ff_v"]), (vraw[:, 1, :], a["fc1_v"]),
                 (vraw[:, 2, :], a["fc2_v"]), (gcol[:, 0:1], col(a["ff_g"])), (gcol[:, 1:2], col(a["fc1_g"])),
                 (gcol[:, 2:3], col(a["fc2_g"])), (ffb[:, :], a["ff_b"].partition_broadcast(P)),
                 (fc2b[:, :], a["fc2_b"].partition_broadcast(P)), (ind_h[:, :], a["ind_h"]),
                 (ind_g[:, :], a["ind_g"]), (negm[:, :], a["negm"])]
        NLOADS = 16 * len(loads)
        rows = z1.rearrange("b h w c -> (b h) w c")

        block = ctx.enter_context(nc.Block())

        @block.sync
        def _(sp):
            for dst, src in loads:
                sp.dma_start(dst, src).then_inc(win, 16)

            def store(n, s):
                at, done = sp.snap(n), sp.snap(n + 1)
                sp.wait_ge(fin_d, done)
                sp.dma_start(out[ds(at, 1)].rearrange("o w n -> w (o n)"),
                             outb[:, s].rearrange("p g n -> p (g n)")).then_inc(out_done[s], 16)

            def load(dst, step, read, got):
                src = rows[ds(sp.snap(step.n * 4), 4)].rearrange("r w c -> w r c")
                if not isinstance(step.n, int) or step.n > 1:
                    value = sp.snap(step.n - 1)
                    sp.wait_ge(read, value)
                sp.dma_start(dst[:, step.s], src).then_inc(got[step.s], 16)

            def body(sp_, sa, sb_, sc):
                if sp_:
                    load(zin, sp_, u_p, zin_in)
                if sb_:
                    load(zres, sb_, zresb_p, zres_in)
                if sc and (not isinstance(sc.n, int) or sc.n > 0):
                    store(sc.n - 1, 1 - sc.s)
                if not (sp_ or sa or sb_ or sc):
                    store(QUADS - 1, 1)

            pipeline(sp, QUADS, body)
            for s in range(2):
                sp.wait_ge(out_done[s], 16 * QUADS // 2)

        @block.gpsimd
        def _(pool):
            pool.memset(mhalf[:, :], -0.5).then_inc(const_p, 1)
            pool.wait_ge(win, NLOADS)
            pool.tensor_copy(ident_b[:, :], ident[:, :]).then_inc(const_p, 1)
            pool.wait_ge(const_p, 2)
            pool.wait_ge(vsq_ready, 3)
            pool.tensor_tensor(vsq[:, :], vsq[:, :], mhalf[:, 0:3], ALU.pow).then_inc(vrs_ready, 1)
            pool.wait_ge(vrs_ready, 1)
            pool.tensor_tensor(gcol[:, :], gcol[:, :], vsq[:, :], ALU.mult).then_inc(vrs_ready, 1)

            def rsqrt(dst, src, scale, eps, src_sem, src_count, sum_sem, root_sem, n):
                pool.wait_ge(src_sem, src_count)
                pool.sem_inc(waited)
                if scale is None:
                    pool.tensor_scalar(dst, src, eps, None, ALU.add).then_inc(sum_sem, 1)
                else:
                    pool.tensor_scalar(dst, src, scale, eps, ALU.mult, ALU.add).then_inc(sum_sem, 1)
                pool.wait_ge(sum_sem, n + 1)
                pool.tensor_tensor(dst, dst, mhalf[:, 0:4], ALU.pow).then_inc(root_sem, 1)

            def add_tap(a_, j):
                pool.wait_ge(conv_d, a_.n * TAPS_D + (2 * j + 2))
                pool.tensor_tensor(acc[:, j, :, 1:], acc[:, j, :, 1:], tap1[:, j, :, 0:P - 1], ALU.add).then_inc(add_p, 1)

            def body(sp_, sa, sb_, sc):
                if sp_:
                    n = sp_.n
                    rsqrt(r1[:, :], mv1[:, :, 1], None, EPS1, mv1_d, n + 1, r1a_p, r1_p, n)
                    later(pool.wait_ge, ut_mm, n)
                    pool.wait_ge(r1_p, n + 1)
                    pool.sem_inc(waited)
                    for g in range(4):
                        ins = pool.tensor_scalar(u[:, g, :], zin[:, sp_.s, g, :], mv1[:, g, 0:1], r1[:, g:g + 1],
                                                 ALU.subtract, ALU.mult)
                    ins.then_inc(u_p, 1)
                if sc:
                    rsqrt(ry[:, sc.s, :], ss[:, sc.s, :], 1.0 / DINNER, EPS1, sq_a, sc.n * 4 + 4, rya_p, ry_p, sc.n)
                    if sa:
                        add_tap(sa, 0)
                    rsqrt(r2[:, :], mv2[:, :, 1], None, EPS1, mv2_d, sc.n + 1, r2a_p, r2_p, sc.n)
                    later(pool.wait_ge, fin_d, sc.n)
                    pool.tensor_tensor(z2b[:, :, :], z2[:, :, :], fc2b[:, :].unsqueeze(1).to_broadcast([P, 4, P]),
                                       ALU.add).then_inc(z2b_p, 1)
                if sb_:
                    pool.wait_ge(zres_in[sb_.s], sb_.half * 16 + 16)
                    later(pool.wait_ge, z2_d, sb_.n)
                    pool.tensor_tensor(zresb[:, :, :], zres[:, sb_.s], ffb[:, :].unsqueeze(1).to_broadcast([P, 4, P]),
                                       ALU.add).then_inc(zresb_p, 1)
                if sa:
                    if not sc:
                        add_tap(sa, 0)
                    add_tap(sa, 1)
                    pool.wait_ge(add_p, sa.n * 2 + 2)
                    pool.wait_ge(q_d, sa.n + 1)
                    later(pool.wait_ge, d_mm, sa.n * 4)
                    pool.tensor_tensor(l4[64:P], q[64:P, :].bitcast(FP).unsqueeze(1).to_broadcast([64, 4, P]),
                                       ind_g[64:P, :].unsqueeze(2).to_broadcast([64, 4, P]), ALU.mult).then_inc(l4_p, 1)
                    pool.wait_ge(l4_p, sa.n + 1)

            pipeline(pool, QUADS, body)

        @block.tensor
        def _(pe):
            pe.wait_ge(win, NLOADS)
            pe.wait_ge(vn_ready, 3)
            for n in range(3):
                pe.transpose(ps[:, 0, n * P:(n + 1) * P], vn[:, n, :], ident[:, :]).then_inc(wt_mm, 1)
            pe.wait_ge(wt_ready, 1)
            for j in range(2):
                pe.matmul(ps[:, 1, j * P:(j + 1) * P], op_raw[:, j * P:(j + 1) * P], wt[:, 0, :],
                          start=True, stop=True).then_inc(wc_mm, 1)
            pe.wait_ge(wc_ready, 2)
            pe.wait_ge(const_p, 2)
            pe.wait_ge(const_d, 3)
            pe.wait_ge(const_a, 2)

            def turn_yg(c, half):
                if half == 0:
                    pe.wait_ge(gate_d, c.n * 4 + 4)
                else:
                    pe.wait_ge(ygt_d, c.n * 2 + 1)
                for k in range(4):
                    g, j = 2 * half + k // 2, k % 2
                    mm = pe.transpose(ps[:, 0, k * P:(k + 1) * P], yg[:, c.s, g, j * P:(j + 1) * P], ident[:, :])
                mm.then_inc(ygt_mm, 1)

            def decays(b, g):
                if g == 0:
                    pe.wait_ge(rz_d, b.n + 1)
                    pe.wait_ge(l4_p, b.n + 1)
                later(pe.wait_ge, e_a, b.n * 4 + g)
                for half in range(2):
                    dst = four(ps[:, 4 + half, :])
                    pe.matmul(dst, l4[:, g, :], rz[:, 4 * half:4 * half + 4, :], start=True, stop=False)
                    mm = pe.matmul(dst, ident_b[:, :], mask_b[:, :].unsqueeze(1).to_broadcast([P, 4, P]),
                                   start=False, stop=True)
                mm.then_inc(d_mm, 1)

            def turn_x(b, pair):
                if pair == 0:
                    pe.wait_ge(xs_a, b.n + 1)
                    later(pe.wait_ge, dtx_d, b.n * 2)
                else:
                    pe.wait_ge(dtx_d, b.n * 2 + 1)
                for k in range(4):
                    mm = pe.transpose(ps[:, 7, k * P:(k + 1) * P], xs[:, b.s, k % 2, 2 * pair + k // 2, :], ident[:, :])
                mm.then_inc(xt_mm, 1)

            def mix(b, g):
                pe.wait_ge(m_d, b.n * 4 + (g + 1))
                pe.wait_ge(dtx_d, b.n * 2 + (g // 2 + 1))
                later(pe.wait_ge, gate_d, b.n * 4 + g)
                for j in range(2):
                    pe.matmul(ps[:, 6, j * P:(j + 1) * P], xs[:, b.s, j, g, :], diag[:, j, :], start=(j == 0), stop=False)
                for h in range(HEADS):
                    at = (g % 2) * DINNER + HEADDIM * h
                    mm = pe.matmul(ps[:, 6, HEADDIM * h:HEADDIM * (h + 1)], mmat[:, g % 2, h * P:(h + 1) * P],
                                   dtx[:, g // 2, at:at + HEADDIM], start=False, stop=(h == HEADS - 1))
                mm.then_inc(y_mm, 1)

            def project(j, bank):
                pe.matmul(ps[:, bank, :], wx[:, j * P:(j + 1) * P], ut[:, :], start=True, stop=True).then_inc(x_mm, 1)

            def gates(pair, bank):
                for k in range(2):
                    g = 2 * pair + k
                    mm = pe.matmul(ps[:, bank, k * DINNER:(k + 1) * DINNER], ut[:, g * P:(g + 1) * P], wz[:, :],
                                   start=True, stop=True)
                mm.then_inc(z_mm, 1)

            def body(sp_, sa, sb_, sc):
                if sb_:
                    pe.wait_ge(bc_a, sb_.n + 1)
                    pe.wait_ge(q_d, sb_.n + 1)
                    for g in range(4):
                        mm = pe.matmul(ps[:, 3, g * P:(g + 1) * P], bmat[:, sb_.s, g, :], cmat[:, sb_.s, g, :],
                                       start=True, stop=True)
                    mm.then_inc(cb_mm, 1)
                    turn_x(sb_, 0)
                if sa:
                    pe.wait_ge(ut_a, sa.n + 1)
                elif sc:
                    pe.wait_ge(zs_a, 2 * QUADS)
                if sc:
                    turn_yg(sc, 0)
                if sa:
                    later(pe.wait_ge, zs_a, sa.n * 2)
                    project(0, 1)
                if sc:
                    turn_yg(sc, 1)
                if sa:
                    if sb_:
                        pe.wait_ge(dtx_d, sb_.n * 2 + 1)
                    for g in range(4):
                        mm = pe.matmul(ps[:, 7, HEADS * g:HEADS * (g + 1)], ut[:, g * P:(g + 1) * P], wdt[:, :],
                                       start=True, stop=True)
                    mm.then_inc(dt_mm, 1)
                if sb_:
                    decays(sb_, 1)
                if sc:
                    pe.wait_ge(ygt_d, sc.n * 2 + 2)
                    later(pe.wait_ge, fin_d, sc.n)
                    for g in range(4):
                        for j in range(2):
                            mm = pe.matmul(ps[:, 2, g * P:(g + 1) * P], ygt[:, g, j, :], wc[:, j, :],
                                           start=(j == 0), stop=(j == 1))
                    mm.then_inc(o_mm, 1)
                if sb_:
                    mix(sb_, 0)
                    if sa:
                        pe.wait_ge(v_d, sa.n + 1)
                    turn_x(sb_, 1)
                    decays(sb_, 2)
                    mix(sb_, 1)
                if sa:
                    if sc:
                        pe.wait_ge(z2_d, sc.n + 1)
                    project(1, 2)
                if sb_:
                    decays(sb_, 3)
                if sa:
                    pe.wait_ge(conv_d, sa.n * TAPS_D + 2)
                    project(2, 1)
                if sb_:
                    mix(sb_, 2)
                if sc:
                    pe.wait_ge(hn_d, sc.n + 1)
                    for g in range(4):
                        mm = pe.transpose(ps[:, 0, g * P:(g + 1) * P], hn[:, g, :], ident[:, :])
                    mm.then_inc(ht_mm, 1)
                if sa:
                    pe.wait_ge(dta_d, sa.n + 1)
                    later(pe.wait_ge, m_d, sa.n * 4)
                    pe.matmul(ps[:, 3, 0:P], dta[:, sa.s].rearrange("p r n -> p (r n)"), tri[:, :],
                              start=True, stop=True).then_inc(cs_mm, 1)
                if sb_:
                    mix(sb_, 3)
                if sc:
                    if sa:
                        pe.wait_ge(conv_d, sa.n * TAPS_D + 4)
                    pe.wait_ge(ht_a, sc.n + 1)
                    pe.matmul(ps[:, 2, :], wt[:, 1, :], ht[:, :], start=True, stop=True).then_inc(f1_mm, 1)
                if sa:
                    gates(1, 0)
                    pe.wait_ge(conv_d, sa.n * TAPS_D + TAPS_D)
                    gates(0, 1)
                if sc:
                    pe.wait_ge(gl_a, sc.n + 1)
                    for g in range(4):
                        mm = pe.matmul(ps[:, 2, g * P:(g + 1) * P], gl[:, g * P:(g + 1) * P], wt[:, 2, :],
                                       start=True, stop=True)
                    mm.then_inc(f2_mm, 1)
                if sp_:
                    later(pe.wait_ge, zs_a, sp_.n * 2 - 1)
                    pe.wait_ge(u_p, sp_.n + 1)
                    for g in range(4):
                        mm = pe.transpose(ps[:, 0, g * P:(g + 1) * P], u[:, g, :], ident[:, :])
                    mm.then_inc(ut_mm, 1)
                if sa:
                    decays(sa, 0)

            pipeline(pe, QUADS, body)

        @block.scalar
        def _(act):
            act.wait_ge(win, NLOADS)
            act.activation(aexp[:, :], alog[:, :], ACT.Exp).then_inc(a_ready, 1)
            for n in range(3):
                act.activation(vn[:, n, :], vraw[:, n, :], ACT.Square, accum_out=vsq[:, n:n + 1]).then_inc(vsq_ready, 1)
            act.wait_ge(wt_mm, 3)
            act.activation(wt[:, :, :].rearrange("p n k -> p (n k)"), ps[:, 0, 0:3 * P], ACT.Copy).then_inc(wt_ready, 1)
            act.wait_ge(wc_mm, 2)
            for j in range(2):
                act.activation(wc[:, j, :], ps[:, 1, j * P:(j + 1) * P], ACT.Copy, scale=ssm_w[:, j:j + 1]).then_inc(wc_ready, 1)
            act.activation(rz[64:P, :, :], ind_h[64:P, :].unsqueeze(2).to_broadcast([64, HEADS, P]),
                           ACT.Copy).then_inc(const_a, 1)
            act.activation(l4[0:64, :, :], ind_g[0:64, :].unsqueeze(2).to_broadcast([64, 4, P]),
                           ACT.Copy).then_inc(const_a, 1)

            def exps(b, g):
                act.wait_ge(d_mm, b.n * 4 + (g + 1))
                later(act.wait_ge, m_d, b.n * 4 + (g - 1))
                act.activation(emat[:, g % 2, :].rearrange("p (b n) -> p b n", b=2), ps[:, 4:6, :], ACT.Exp).then_inc(e_a, 1)

            def first_tap(a_, j, bank):
                act.wait_ge(x_mm, a_.n * 3 + (j + 1))
                act.activation(acc[:, j], four(ps[:, bank, :]), ACT.Identity, bias=conv_b[:, j:j + 1],
                               scale=conv_w[:, j, 3:4]).then_inc(tap_a, 1)
                if j < 2:
                    act.activation(tap1[:, j], four(ps[:, bank, :]), ACT.Identity,
                                   scale=conv_w[:, j, 2:3]).then_inc(tap_a, 1)

            def squares(b, g):
                act.wait_ge(gate_d, b.n * 4 + (g + 1))
                later(act.wait_ge, sq_a, b.n * 4 + g)
                act.activation(junk[:, :], yg[:, b.s, g, :], ACT.Square, accum_out=ss[:, b.s, g:g + 1]).then_inc(sq_a, 1)

            def gates(a_, nth, pair, bank):
                act.wait_ge(z_mm, a_.n * 2 + (nth + 1))
                act.activation(zs[:, a_.s, 2 * pair:2 * pair + 2].rearrange("p g n -> p (g n)"), ps[:, bank, :],
                               ACT.Silu).then_inc(zs_a, 1)

            def body(sp_, sa, sb_, sc):
                if sa:
                    act.wait_ge(ut_mm, sa.n + 1)
                    act.activation(ut[:, :], ps[:, 0, :], ACT.Identity, bias=lncol[:, 1:2], scale=lncol[:, 0:1]).then_inc(ut_a, 1)
                if sb_:
                    gates(sb_, 1, 0, 1)
                act.preload_act_table_set("natural_log_exp_and_others")
                if sb_:
                    exps(sb_, 0)
                if sa:
                    first_tap(sa, 0, 1)
                if sc:
                    squares(sc, 3)
                if sb_:
                    exps(sb_, 1)
                if sa:
                    act.wait_ge(vabs_d, sa.n + 1)
                    act.activation(ve[:, :], vabs[:, :], ACT.Exp, scale=-1.0).then_inc(ve_a, 1)
                if sb_:
                    exps(sb_, 2)
                    squares(sb_, 0)
                if sa:
                    act.wait_ge(vu_d, sa.n + 1)
                    act.activation(vl[:, :], vu[:, :], ACT.Ln).then_inc(vl_a, 1)
                    first_tap(sa, 1, 2)
                if sb_:
                    exps(sb_, 3)
                if sa:
                    first_tap(sa, 2, 1)
                if sb_:
                    squares(sb_, 1)
                if sc:
                    act.wait_ge(ht_mm, sc.n + 1)
                    act.activation(ht[:, :], ps[:, 0, :], ACT.Identity, bias=lncol[:, 3:4], scale=lncol[:, 2:3]).then_inc(ht_a, 1)
                    act.wait_ge(f1_mm, sc.n + 1)
                    act.activation(gl[:, :], ps[:, 2, :], ACT.Gelu, bias=fc1_b[:, :]).then_inc(gl_a, 1)
                if sb_:
                    squares(sb_, 2)
                if sa:
                    gates(sa, 0, 1, 0)
                    act.wait_ge(conv_d, sa.n * TAPS_D + TAPS_D)
                    act.activation(bmat[:, sa.s], acc[0:64, 2], ACT.Silu)
                    act.activation(cmat[:, sa.s], acc[64:P, 2], ACT.Silu).then_inc(bc_a, 1)
                    act.wait_ge(add_p, sa.n * 2 + 2)
                    act.activation(xs[:, sa.s], acc[:, 0:2], ACT.Silu).then_inc(xs_a, 1)

            pipeline(act, QUADS, body)

        @block.vector
        def _(dve):
            dve.wait_ge(win, NLOADS)
            dve.tensor_scalar(mask_b[:, :], tri[:, :], -1.0, BIG, ALU.add, ALU.mult).then_inc(const_d, 1)
            dve.wait_ge(a_ready, 1)
            dve.tensor_scalar(amat[:, :].rearrange("p (g h) -> p g h", g=4),
                              aexp[:, :].unsqueeze(1).to_broadcast([P, 4, HEADS]), -1.0, None, ALU.mult).then_inc(const_d, 1)
            for j in range(2):
                ins = dve.tensor_scalar(diag[:, j, :], ident[:, :], dcol[:, j:j + 1], None, ALU.mult)
            ins.then_inc(const_d, 1)
            dve.wait_ge(vrs_ready, 2)
            for n in range(3):
                dve.tensor_scalar(vn[:, n, :], vraw[:, n, :], gcol[:, n:n + 1], None, ALU.mult).then_inc(vn_ready, 1)
            dve.wait_ge(const_d, 3)
            dve.wait_ge(const_a, 2)

            def pair_dtx(b, pair):
                dve.wait_ge(xt_mm, b.n * 2 + (pair + 1))
                later(dve.wait_ge, y_mm, b.n * 4 + (2 * pair - 2))
                dve.tensor_tensor(dtx[:, pair, :].rearrange("p (n d) -> p n d", d=HEADDIM),
                                  ps[:, 7, :].rearrange("p (n d) -> p n d", d=HEADDIM),
                                  dt[:, b.s, 16 * pair:16 * pair + 16].unsqueeze(2).to_broadcast([P, 16, HEADDIM]),
                                  ALU.mult).then_inc(dtx_d, 1)

            def weigh(b, g):
                dve.wait_ge(e_a, b.n * 4 + (g + 1))
                dve.wait_ge(cb_mm, b.n + 1)
                later(dve.wait_ge, y_mm, b.n * 4 + (g - 1))
                dve.tensor_tensor(mmat[:, g % 2, :].rearrange("p (h n) -> p h n", h=HEADS),
                                  emat[:, g % 2, :].rearrange("p (h n) -> p h n", h=HEADS),
                                  ps[:, 3, g * P:(g + 1) * P].unsqueeze(1).to_broadcast([P, HEADS, P]),
                                  ALU.mult).then_inc(m_d, 1)

            def taps(a_, j, bank):
                dve.wait_ge(tap_a, a_.n * TAPS_A + min(2 * j + 2, TAPS_A))
                for k in range(2 if j < 2 else 1, 4):
                    if k > (2 if j < 2 else 1):
                        dve.wait_ge(conv_d, a_.n * TAPS_D + (2 * j + k - (2 if j < 2 else 1)))
                    dve.scalar_tensor_tensor(out=acc[:, j, :, k:], in0=four(ps[:, bank, :])[:, :, 0:P - k],
                                             scalar=conv_w[:, j, 3 - k:4 - k], in1=acc[:, j, :, k:],
                                             op0=ALU.mult, op1=ALU.add).then_inc(conv_d, 1)

            def copy_ygt(c, half):
                dve.wait_ge(ygt_mm, c.n * 2 + (half + 1))
                dve.tensor_copy(ygt[:, 2 * half:2 * half + 2].rearrange("p g j n -> p (g j n)"),
                                ps[:, 0, :]).then_inc(ygt_d, 1)

            def gate(b, g):
                dve.wait_ge(y_mm, b.n * 4 + (g + 1))
                dve.wait_ge(zs_a, b.n * 2 + 2)
                dve.tensor_tensor(yg[:, b.s, g, :], ps[:, 6, 0:DINNER], zs[:, b.s, g, :], ALU.mult).then_inc(gate_d, 1)

            def moments(src, st, mv, st_sem, mv_sem, n):
                for g in range(4):
                    ins = dve.bn_stats(st[:, g, :], src[:, g, :])
                ins.then_inc(st_sem, 1)
                dve.wait_ge(st_sem, n + 1)
                dve.sem_inc(waited)
                for g in range(4):
                    ins = dve.bn_aggr(mv[:, g, :], st[:, g, :])
                ins.then_inc(mv_sem, 1)

            def norm(dst, src, mv, r):
                for g in range(4):
                    ins = dve.tensor_scalar(dst[:, g, :], src[:, g, :], mv[:, g, 0:1], r[:, g:g + 1],
                                            ALU.subtract, ALU.mult)
                return ins

            def body(sp_, sa, sb_, sc):
                if sp_:
                    n = sp_.n
                    dve.wait_ge(zin_in[sp_.s], sp_.half * 16 + 16)
                    later(dve.wait_ge, u_p, n)
                    moments(zin[:, sp_.s], st1, mv1, st1_d, mv1_d, n)
                if sc:
                    copy_ygt(sc, 0)
                if sb_:
                    pair_dtx(sb_, 0)
                if sc:
                    copy_ygt(sc, 1)
                if sb_:
                    weigh(sb_, 0)
                if sa:
                    n = sa.n
                    dve.wait_ge(dt_mm, n + 1)
                    dve.tensor_tensor(v[:, :].rearrange("p (g h) -> p g h", g=4),
                                      ps[:, 7, 0:HD].rearrange("p (g h) -> p g h", g=4),
                                      dtb[:, :].unsqueeze(1).to_broadcast([P, 4, HEADS]), ALU.add).then_inc(v_d, 1)
                    dve.wait_ge(v_d, n + 1)
                    dve.scalar_tensor_tensor(out=vabs[:, :], in0=v[:, :], scalar=-1.0, in1=v[:, :],
                                             op0=ALU.mult, op1=ALU.max).then_inc(vabs_d, 1)
                if sa:
                    taps(sa, 0, 1)
                    dve.wait_ge(ve_a, sa.n + 1)
                    dve.tensor_scalar(vu[:, :], ve[:, :], 1.0, None, ALU.add).then_inc(vu_d, 1)
                if sb_:
                    weigh(sb_, 1)
                    gate(sb_, 0)
                if sc:
                    n = sc.n
                    dve.wait_ge(o_mm, n + 1)
                    dve.wait_ge(zresb_p, n + 1)
                    dve.wait_ge(ry_p, n + 1)
                    later(dve.wait_ge, z2b_p, n)
                    for g in range(4):
                        ins = dve.scalar_tensor_tensor(out=z2[:, g, :], in0=ps[:, 2, g * P:(g + 1) * P],
                                                       scalar=ry[:, sc.s, g:g + 1], in1=zresb[:, g, :],
                                                       op0=ALU.mult, op1=ALU.add)
                    ins.then_inc(z2_d, 1)
                    dve.wait_ge(z2_d, n + 1)
                    moments(z2, st2, mv2, st2_d, mv2_d, n)
                if sb_:
                    weigh(sb_, 2)
                    pair_dtx(sb_, 1)
                    gate(sb_, 1)
                if sa:
                    n = sa.n
                    dve.wait_ge(vl_a, n + 1)
                    dve.wait_ge(vu_d, n + 1)
                    dve.scalar_tensor_tensor(out=vr[:, :], in0=vu[:, :], scalar=-1.0, in1=ve[:, :],
                                             op0=ALU.add, op1=ALU.subtract).then_inc(vr_d, 1)
                    dve.scalar_tensor_tensor(out=vx[:, :], in0=v[:, :], scalar=0.0, in1=vl[:, :],
                                             op0=ALU.max, op1=ALU.add).then_inc(vx_d, 1)
                    dve.wait_ge(vr_d, n + 1)
                    dve.wait_ge(vx_d, n + 1)
                    dve.tensor_tensor(dt[:, sa.s, :], vx[:, :], vr[:, :], ALU.subtract).then_inc(dt_d, 1)
                    dve.wait_ge(dt_d, n + 1)
                    dve.tensor_tensor(dta[:, sa.s], dt[:, sa.s, :].unsqueeze(1).to_broadcast([P, 4, HD]),
                                      amat[:, :].unsqueeze(1).to_broadcast([P, 4, HD]), ALU.mult).then_inc(dta_d, 1)
                if sc:
                    dve.wait_ge(mv2_d, sc.n + 1)
                    dve.wait_ge(r2_p, sc.n + 1)
                    norm(hn, z2, mv2, r2).then_inc(hn_d, 1)
                if sb_:
                    weigh(sb_, 3)
                    gate(sb_, 2)
                if sa:
                    taps(sa, 1, 2)
                if sa:
                    taps(sa, 2, 1)
                if sb_:
                    gate(sb_, 3)
                if sa:
                    n = sa.n
                    dve.wait_ge(cs_mm, n + 1)
                    dve.tensor_copy(hi4[:, :], ps[:, 3, 0:P]).then_inc(hi4_d, 1)
                    dve.wait_ge(hi4_d, n + 1)
                    later(dve.wait_ge, l4_p, n)
                    dve.scalar_tensor_tensor(out=q[:, :], in0=hi4[:, :].bitcast(FP), scalar=negm[:, 0:1], in1=ps[:, 3, 0:P],
                                             op0=ALU.mult, op1=ALU.add).then_inc(q_d, 1)
                    dve.wait_ge(q_d, n + 1)
                    later(dve.wait_ge, d_mm, n * 4)
                    dve.tensor_tensor(rz[0:64], q[0:64, :].bitcast(FP).unsqueeze(1).to_broadcast([64, HEADS, P]),
                                      ind_h[0:64, :].unsqueeze(2).to_broadcast([64, HEADS, P]), ALU.mult).then_inc(rz_d, 1)
                if sc:
                    n = sc.n
                    dve.wait_ge(f2_mm, n + 1)
                    dve.wait_ge(z2b_p, n + 1)
                    later(dve.wait_ge, out_done[sc.s], sc.half * 16)
                    dve.tensor_tensor(outb[:, sc.s], four(ps[:, 2, :]), z2b[:, :, :], ALU.add).then_inc(fin_d, 1)

            pipeline(dve, QUADS, body)


def step_tables():
    import numpy as np
    p = np.arange(P)
    f = lambda m: np.ascontiguousarray(m, dtype=np.float32)
    sign = np.where(p < 64, 1.0, -1.0)[:, None]
    return {"tri": f(np.triu(np.ones((P, P)))),
            "ind_h": f(p[:, None] % HEADS == np.arange(HEADS)),
            "ind_g": f(sign * (p[:, None] % 32 // HEADS == np.arange(4))),
            "negm": f(-(p[:, None] // 32 % 2))}


def kernel(**inputs):
    import numpy as np
    import concourse.bacc as _bacc
    from concourse.bass_utils import run_bass_kernel_spmd as _run

    x = np.asarray(inputs["x"])
    arrays = {"x": x,
              "x_cols": x.transpose(0, 1, 3, 2).reshape(IMAGES, H, C // 4, 4 * W).transpose(0, 2, 1, 3)
                         .reshape(IMAGES * C // 4, H, 4 * W)}
    for n in ("w_h", "b_h", "w_l", "b_l", "b_f", "gamma", "beta"):
        arrays[n] = np.asarray(inputs["L0_conv_" + n])
    arrays["w_f"] = np.asarray(inputs["L0_conv_w_f"]).reshape(9, C, C)
    for n in ("ln1_w", "ln1_b", "ln2_w", "ln2_b", "conv_w", "dt_bias", "A_log", "out_proj_w",
              "ff_g", "ff_v", "ff_b", "fc1_g", "fc1_v", "fc1_b", "fc2_g", "fc2_v", "fc2_b"):
        arrays[n] = np.asarray(inputs["L1_conv_" + n])
    arrays["in_proj_t"] = np.asarray(inputs["L1_conv_in_proj_w"]).T
    arrays["conv_b3"] = np.asarray(inputs["L1_conv_conv_b"]).reshape(3, P).T
    arrays["d_cols"] = np.repeat(np.asarray(inputs["L1_conv_D_param"]), HEADDIM).reshape(2, P).T
    arrays["ssm_w2"] = np.asarray(inputs["L1_conv_ssm_norm_w"]).reshape(2, P).T
    arrays.update(dft_tables())
    arrays.update(step_tables())

    nc = _bacc.Bacc("TRN2", target_bir_lowering=False, num_devices=1)
    arrays = {"in_" + n: np.ascontiguousarray(v) for n, v in arrays.items()}
    a = {n[3:]: nc.dram_tensor(n, v.shape, FP, kind="ExternalInput").ap() for n, v in arrays.items()}
    z1 = nc.dram_tensor("z1", (IMAGES, H, W, C), FP, kind="Internal").ap()
    out = nc.dram_tensor("out", (QUADS, W, 4 * C), FP, kind="ExternalOutput").ap()
    spectral_block(nc, a, z1)
    sequence_block(nc, a, z1, out)
    r = _run(nc, [arrays], core_ids=[0])
    got = np.asarray(r.results[0]["out"])
    return got.reshape(IMAGES, H // 4, W, 4, C).transpose(0, 1, 3, 2, 4).reshape(IMAGES, H, W, C)
```
